# Optimizing a Trainium2 kernel written in Bass

```python
import numpy as np
import jax
import jax.numpy as jnp

def _softmax(x, axis=-1):
    return jax.nn.softmax(x, axis=axis)

def _gelu(x):
    return jax.nn.gelu(x, approximate=True)

def _silu(x):
    return jax.nn.silu(x)

def _sigmoid(x):
    return jax.nn.sigmoid(x)

def _layernorm(x, axis=-1, eps=1e-05):
    m = jnp.mean(x, axis=axis, keepdims=True)
    v = jnp.var(x, axis=axis, keepdims=True)
    return (x - m) / jnp.sqrt(v + eps)

def _scatter_add(tgt, idx, src, axis=0):
    return tgt.at[idx].add(src)

def _segment_sum(src, seg, n):
    return jax.ops.segment_sum(src, seg, n)
kernel_name = 'mk_early_fusion_d1_tok_img1024_r4_64d3b9'

def setup_inputs(seed: int=0):
    np.random.seed(seed)
    _w = jnp.asarray

    def _rec_inputs():
        import jax
        import jax.numpy as jnp
        _rk = jax.random.key(seed)
        x = -0.000125008 + 0.999885 * jax.random.normal(jax.random.fold_in(_rk, 1), (8, 512, 256, 4), jnp.float32)
        txt = -8.03667e-05 + 0.656214 * jax.random.normal(jax.random.fold_in(_rk, 2), (8, 77, 256), jnp.float32)
        return (x, txt)
    x, txt = _rec_inputs()

    def _L0_tok_setup():
        import jax, jax.numpy as jnp
        import numpy as np
        key = jax.random.key(seed)
        k1, k2, k3 = jax.random.split(key, 3)
        B, H, I, O, Dp1 = (4, 512, 256, 256, 4)
        x = jax.random.normal(k1, (B, H, I, Dp1), dtype=jnp.float32)
        weight = 0.1 * jax.random.normal(k2, (O, Dp1), dtype=jnp.float32)
        weighted_sum = 0.1 * jax.random.normal(k3, (O, I), dtype=jnp.float32)
        return {'x': x, 'weight': weight, 'weighted_sum': weighted_sum}
    _L0_tok_all = _L0_tok_setup()
    _L0_tok_in = {k: v for k, v in _L0_tok_all.items() if k in ('weight', 'weighted_sum')}
    del _L0_tok_all

    def _L0_attn_setup():
        import jax, jax.numpy as jnp
        import numpy as np
        import math
        DIM = 256
        NUM_HEADS = 16
        HEAD_DIM = DIM // NUM_HEADS
        LOGIT_SCALE_MAX = math.log(1.0 / 0.01)
        EPS = 1e-12

        def _l2_normalize(t):
            n = jnp.sqrt(jnp.sum(t * t, axis=-1, keepdims=True))
            return t / jnp.maximum(n, EPS)
        key = jax.random.key(seed)
        ks = jax.random.split(key, 4)
        L, N, C = (256, 8, DIM)
        scale = HEAD_DIM ** (-0.5)
        x = jax.random.normal(ks[0], (L, N, C), dtype=jnp.float32)
        in_proj_weight = jax.random.normal(ks[1], (3 * C, C), dtype=jnp.float32) * scale
        in_proj_bias = jnp.zeros((3 * C,), dtype=jnp.float32)
        logit_scale = jnp.full((NUM_HEADS, 1, 1), math.log(10.0), dtype=jnp.float32)
        head_scale = jnp.ones((NUM_HEADS, 1, 1), dtype=jnp.float32)
        out_w = jax.random.normal(ks[2], (C, C), dtype=jnp.float32) * C ** (-0.5)
        out_b = jax.random.normal(ks[3], (C,), dtype=jnp.float32) * 0.01
        return {'x': x, 'in_proj_weight': in_proj_weight, 'in_proj_bias': in_proj_bias, 'logit_scale': logit_scale, 'head_scale': head_scale, 'out_w': out_w, 'out_b': out_b}
    _L0_attn_all = _L0_attn_setup()
    _L0_attn_in = {k: v for k, v in _L0_attn_all.items() if k in ('in_proj_weight', 'in_proj_bias', 'logit_scale', 'head_scale', 'out_w', 'out_b')}
    del _L0_attn_all

    def _L0_ffn_setup():
        import jax, jax.numpy as jnp
        import numpy as np
        D = 256
        H = 16
        HD = D // H
        L = 64
        E = 8
        B, T = (4, 512)
        EPS = 1e-06

        def _glorot(k, shape):
            fan_in, fan_out = (shape[-2], shape[-1])
            lim = np.sqrt(6.0 / (fan_in + fan_out)).astype(np.float32)
            return jax.random.uniform(k, shape, jnp.float32, -lim, lim)

        def _rmsnorm(x, gamma):
            return gamma * x * jax.lax.rsqrt(jnp.mean(x * x, axis=-1, keepdims=True) + EPS)
        key = jax.random.key(seed)
        ks = jax.random.split(key, 8)
        return {'x': jax.random.normal(ks[0], (B, T, D), jnp.float32), 'gamma1': jnp.ones((D,), jnp.float32), 'Wq': _glorot(ks[1], (D, D)), 'bq': jnp.zeros((D,), jnp.float32), 'Wdown': _glorot(ks[2], (D, L)), 'bdown': jnp.zeros((L,), jnp.float32), 'Wup': _glorot(ks[3], (L, 2 * D)), 'bup': jnp.zeros((2 * D,), jnp.float32), 'Wo': _glorot(ks[4], (D, D)), 'bo': jnp.zeros((D,), jnp.float32), 'gamma2': jnp.ones((D,), jnp.float32), 'Wg': _glorot(ks[5], (D, E)), 'bg': jnp.zeros((E,), jnp.float32), 'We': _glorot(ks[6], (E, D, D))}
    _L0_ffn_all = _L0_ffn_setup()
    _L0_ffn_in = {k: v for k, v in _L0_ffn_all.items() if k in ('gamma1', 'Wq', 'bq', 'Wdown', 'bdown', 'Wup', 'bup', 'Wo', 'bo', 'gamma2', 'Wg', 'bg', 'We')}
    del _L0_ffn_all
    return {'x': x, 'txt': txt, 'L0_tok_weight': _L0_tok_in['weight'], 'L0_tok_weighted_sum': _L0_tok_in['weighted_sum'], 'L0_attn_in_proj_weight': _L0_attn_in['in_proj_weight'], 'L0_attn_in_proj_bias': _L0_attn_in['in_proj_bias'], 'L0_attn_logit_scale': _L0_attn_in['logit_scale'], 'L0_attn_head_scale': _L0_attn_in['head_scale'], 'L0_attn_out_w': _L0_attn_in['out_w'], 'L0_attn_out_b': _L0_attn_in['out_b'], 'L0_ffn_gamma1': _L0_ffn_in['gamma1'], 'L0_ffn_Wq': _L0_ffn_in['Wq'], 'L0_ffn_bq': _L0_ffn_in['bq'], 'L0_ffn_Wdown': _L0_ffn_in['Wdown'], 'L0_ffn_bdown': _L0_ffn_in['bdown'], 'L0_ffn_Wup': _L0_ffn_in['Wup'], 'L0_ffn_bup': _L0_ffn_in['bup'], 'L0_ffn_Wo': _L0_ffn_in['Wo'], 'L0_ffn_bo': _L0_ffn_in['bo'], 'L0_ffn_gamma2': _L0_ffn_in['gamma2'], 'L0_ffn_Wg': _L0_ffn_in['Wg'], 'L0_ffn_bg': _L0_ffn_in['bg'], 'L0_ffn_We': _L0_ffn_in['We']}

def reference(x, txt, L0_tok_weight, L0_tok_weighted_sum, L0_attn_in_proj_weight, L0_attn_in_proj_bias, L0_attn_logit_scale, L0_attn_head_scale, L0_attn_out_w, L0_attn_out_b, L0_ffn_gamma1, L0_ffn_Wq, L0_ffn_bq, L0_ffn_Wdown, L0_ffn_bdown, L0_ffn_Wup, L0_ffn_bup, L0_ffn_Wo, L0_ffn_bo, L0_ffn_gamma2, L0_ffn_Wg, L0_ffn_bg, L0_ffn_We):
    import jax
    import jax.numpy as jnp

    def _L0_tok_ref(x, weight, weighted_sum):
        import jax, jax.numpy as jnp
        import numpy as np
        return jnp.einsum('bhid,oi,od->bho', x, weighted_sum, weight)

    def _L0_attn_ref(x, in_proj_weight, in_proj_bias, logit_scale, head_scale, out_w, out_b):
        import jax, jax.numpy as jnp
        import numpy as np
        import math
        DIM = 256
        NUM_HEADS = 16
        HEAD_DIM = DIM // NUM_HEADS
        LOGIT_SCALE_MAX = math.log(1.0 / 0.01)
        EPS = 1e-12

        def _l2_normalize(t):
            n = jnp.sqrt(jnp.sum(t * t, axis=-1, keepdims=True))
            return t / jnp.maximum(n, EPS)
        L, N, C = x.shape
        H, hd = (NUM_HEADS, HEAD_DIM)
        qkv = x @ in_proj_weight.T + in_proj_bias
        q, k, v = jnp.split(qkv, 3, axis=-1)

        def to_heads(t):
            return t.reshape(L, N, H, hd).transpose(1, 2, 0, 3)
        q, k, v = (to_heads(q), to_heads(k), to_heads(v))
        ls = jnp.exp(jnp.minimum(logit_scale, LOGIT_SCALE_MAX))
        attn = jnp.einsum('nhld,nhmd->nhlm', _l2_normalize(q), _l2_normalize(k)) * ls
        attn = jax.nn.softmax(attn, axis=-1)
        o = jnp.einsum('nhlm,nhmd->nhld', attn, v)
        o = o * head_scale
        o = o.transpose(2, 0, 1, 3).reshape(L, N, C)
        return o @ out_w.T + out_b

    def _L0_ffn_ref(x, gamma1, Wq, bq, Wdown, bdown, Wup, bup, Wo, bo, gamma2, Wg, bg, We):
        import jax, jax.numpy as jnp
        import numpy as np
        D = 256
        H = 16
        HD = D // H
        L = 64
        E = 8
        B, T = (4, 512)
        EPS = 1e-06

        def _glorot(k, shape):
            fan_in, fan_out = (shape[-2], shape[-1])
            lim = np.sqrt(6.0 / (fan_in + fan_out)).astype(np.float32)
            return jax.random.uniform(k, shape, jnp.float32, -lim, lim)

        def _rmsnorm(x, gamma):
            return gamma * x * jax.lax.rsqrt(jnp.mean(x * x, axis=-1, keepdims=True) + EPS)
        b, t = (x.shape[0], x.shape[1])
        h = _rmsnorm(x, gamma1)
        q = (h @ Wq + bq).reshape(b, t, H, HD)
        kv = ((h @ Wdown + bdown) @ Wup + bup).reshape(b, t, H, 2 * HD)
        k, v = jnp.split(kv, 2, axis=-1)
        att = jnp.einsum('bthd,btgd->bthg', q, k) / np.sqrt(HD).astype(np.float32)
        att = jax.nn.softmax(att, axis=-1)
        out = jnp.einsum('bthg,btgd->bthd', att, v).reshape(b, t, D)
        x = x + (out @ Wo + bo)
        h2 = _rmsnorm(x, gamma2)
        gate = jax.nn.softmax(h2 @ Wg + bg, axis=-1)
        combined = jnp.einsum('btd,edf,bte->btf', h2, We, gate)
        return x + combined
    h = _L0_tok_ref(x, L0_tok_weight, L0_tok_weighted_sum)
    h = jnp.concatenate([h, txt], axis=1)
    h = h + _L0_attn_ref(_layernorm(h, axis=-1), L0_attn_in_proj_weight, L0_attn_in_proj_bias, L0_attn_logit_scale, L0_attn_head_scale, L0_attn_out_w, L0_attn_out_b)
    h = h + _L0_ffn_ref(_layernorm(h, axis=-1), L0_ffn_gamma1, L0_ffn_Wq, L0_ffn_bq, L0_ffn_Wdown, L0_ffn_bdown, L0_ffn_Wup, L0_ffn_bup, L0_ffn_Wo, L0_ffn_bo, L0_ffn_gamma2, L0_ffn_Wg, L0_ffn_bg, L0_ffn_We)
    return h

_drawn_inputs = setup_inputs


def setup_inputs(seed=0):
    import zlib

    import numpy as np

    out = dict(_drawn_inputs(seed))
    spreads = {'L0_attn_in_proj_bias': (0.0, 0.1),
     'L0_attn_logit_scale': (2.3025851249694824, 0.2),
     'L0_attn_head_scale': (1.0, 0.2),
     'L0_ffn_gamma1': (1.0, 0.6),
     'L0_ffn_bq': (0.0, 0.8),
     'L0_ffn_bdown': (0.0, 0.8),
     'L0_ffn_bup': (0.0, 0.694),
     'L0_ffn_bo': (0.0, 0.277),
     'L0_ffn_gamma2': (1.0, 0.2),
     'L0_ffn_bg': (0.0, 0.8)}
    factors = {'L0_attn_out_b': 8.0}
    for name, (base, spread) in spreads.items():
        noise = np.random.default_rng([zlib.crc32(name.encode()), seed]).standard_normal(out[name].shape)
        drawn = base * np.exp(spread * noise) if base else spread * noise
        out[name] = jnp.asarray(drawn.astype(out[name].dtype))
    for name, factor in factors.items():
        out[name] = (out[name] * factor).astype(out[name].dtype)
    return out
```

```python
import concourse.bass as bass
from concourse import mybir
from contextlib import ExitStack

F32 = mybir.dt.float32
BF16 = mybir.dt.bfloat16
U32 = mybir.dt.uint32
I32 = mybir.dt.int32
ALU = mybir.AluOpType
ACT = mybir.ActivationFunctionType
AX = mybir.AxisListType

P = 128
B = 8
N_IMG, N_TXT = 512, 77
D = 256
KC = D // P
H, HD = 16, 16
FX = D * 4
XC = FX // P
IMG_TILES = N_IMG * B // P
TOKENS = (N_IMG + N_TXT) * B
TILES = -(-TOKENS // P)
TAIL = TOKENS - (TILES - 1) * P
LAT = 64
E = 8
BIG = float(2 ** 120)
RSQRT_MAGIC = 0x5F3759DF
LN_EPS, RMS_EPS = 1e-5, 1e-6
MEAN, RS, NM, RR = range(4)
XB = 4
NBIAS = 3 * D + D + D + D + E


def wait(eng, sem, value):
    if not isinstance(value, int) or value > 0:
        eng.wait_ge(sem, value)


def settle(eng, sem):
    eng.wait_ge(sem, 1)


def tiles_in_order(eng, body, back, ahead):
    first, end = back + 2, TILES - ahead
    for i in range(-ahead, first):
        body(i)
    with eng.Fori(first, end) as i:
        body(i)
    for i in range(end, TILES + back):
        body(i)


def real(i, k):
    return not isinstance(i, int) or 0 <= i + k < TILES


def build(nc, x, txt, ws_t, w_t, in_w, in_b, logit, head, out_w, out_b, g1, wq, bq, wd, bd, wu, bu,
          wo, bo, g2, wg, bg, we, ident_c, amask_c, fmask_c, pick_c, out):
    ctx = ExitStack()
    with ctx:
        def sb(name, shape, dt=F32):
            return ctx.enter_context(nc.sbuf_tensor(name, shape, dt))

        def sem(name):
            return ctx.enter_context(nc.semaphore(name))

        h_all = sb("h_all", [P, TILES, D])
        cf_all = sb("cf_all", [P, TILES, 4])
        ident = sb("ident", [P, P])
        tokw = sb("tokw", [P, XC, D])
        tokd = sb("tokd", [P, D])
        inw = sb("inw", [P, KC, 3 * D])
        outw = sb("outw", [P, KC, D])
        headw = sb("headw", [P, KC])
        ls = sb("ls", [P, H])
        wq_s = sb("wq_s", [P, KC, D])
        wd_s = sb("wd_s", [P, KC, LAT])
        wu_s = sb("wu_s", [LAT + 1, 2 * D])
        wo_s = sb("wo_s", [P, KC, D])
        wg_s = sb("wg_s", [P, KC, E])
        we_s = sb("we_s", [P, KC, E, D])
        g1_s = sb("g1_s", [P, KC])
        g2_s = sb("g2_s", [P, KC])
        bd_s = sb("bd_s", [LAT, 1])
        bias_f = sb("bias_f", [3, NBIAS])
        bias_l = sb("bias_l", [3, NBIAS])
        bias_p = sb("bias_p", [3, NBIAS], BF16)
        bias_a = sb("bias_a", [3, NBIAS])
        brow = sb("brow", [3, NBIAS], BF16)
        pick = sb("pick", [3, 3])
        ones3 = sb("ones3", [3, P], BF16)
        am_f = sb("am_f", [4, P + 512])
        fm_f = sb("fm_f", [2, P + 512])
        am = sb("am", [4, P + 512], BF16)
        fm = sb("fm", [2, P + 512], BF16)
        neghalf = sb("neghalf", [P, 1])
        ln_eps = sb("ln_eps", [P, 1])
        rms_eps = sb("rms_eps", [P, 1])
        xbuf = [sb(f"xbuf{b}", [P, FX]) for b in range(XB)]
        x_t = [sb(f"x_t{b}", [P, XC, P]) for b in range(2)]
        st = sb("st", [P, 6])
        mv = sb("mv", [P, 2])
        cf = sb("cf", [P, 4])
        vtmp = sb("vtmp", [P, 1])
        xn = sb("xn", [P, D])
        xn_t = sb("xn_t", [P, KC, P])
        sq = sb("sq", [P, 2 * H, HD])
        ss = sb("ss", [P, 2 * H])
        guess = sb("guess", [P, 2 * H])
        rn = sb("rn", [P, 2 * H])
        rt = sb("rt", [P, 2 * H])
        qn = sb("qn", [P, H, HD])
        kpad = sb("kpad", [P, H // 2, 4, HD])
        q_t = sb("q_t", [P, 8, 32])
        k_t = sb("k_t", [P, 8, 64])
        vaug = sb("vaug", [P, H, HD + 1])
        smax = sb("smax", [P, 16])
        sc = sb("sc", [P, 16, 32])
        pr = sb("pr", [P, 16, 32])
        pr_t = sb("pr_t", [P, 16, 32])
        rsum = sb("rsum", [P, H])
        on = sb("on", [P, H, HD])
        on_t = sb("on_t", [P, KC, P])
        hnew = sb("hnew", [P, D])
        ms = sb("ms", [P, 1])
        mse = sb("mse", [P, 1])
        ms2 = sb("ms2", [P, 1])
        x1 = sb("x1", [P, D])
        hn = sb("hn", [P, D])
        hn_t = sb("hn_t", [P, KC, P])
        lat = sb("lat", [LAT + 1, P])
        qpad = sb("qpad", [P, H, 32])
        fq_t = sb("fq_t", [P, 32, H])
        kv_t = sb("kv_t", [P, H, 32])
        v48 = sb("v48", [P, 16, 48])
        of = sb("of", [P, H, 32])
        x2 = sb("x2", [P, D])
        hx2 = sb("hx2", [P, D])
        junk = sb("junk", [P, D])
        ss2 = sb("ss2", [P, 1])
        t2 = sb("t2", [P, 1])
        r2 = sb("r2", [P, 1])
        h2 = sb("h2", [P, D])
        h2_t = sb("h2_t", [P, KC, P])
        gmax = sb("gmax", [P, 1])
        gexp = sb("gexp", [P, E])
        gsum = sb("gsum", [P, 1])
        grec = sb("grec", [P, 1])
        gate = sb("gate", [P, E])
        acc = sb("acc", [P, D])
        res = sb("res", [P, D])

        bank = [ctx.enter_context(nc.psum_tensor(f"bank{n}", [P, 512], F32)) for n in range(8)]

        w_in, tokw_in, c_in, txt_in, txt_zero = (sem(n) for n in ("w_in", "tokw_in", "c_in", "txt_in", "txt_zero"))
        x_in = [sem(f"x_in{b}") for b in range(XB)]
        tokw_ready, consts_ready, link1 = sem("tokw_ready"), sem("consts_ready"), sem("link1")
        front_done, back_done = sem("front_done"), sem("back_done")
        front_ready, back_ready = sem("front_ready"), sem("back_ready")
        mix_done, h_ready, stats_ready, st_link = sem("mix_done"), sem("h_ready"), sem("stats_ready"), sem("st_link")
        c_var, c_rs, c_all = sem("c_var"), sem("c_rs"), sem("c_all")

        with nc.Block() as block:
            @block.sync
            def _(sp):
                sp.dma_start(ident[:, :], ident_c).then_inc(c_in, 16)
                for b in range(XB):
                    sp.dma_start(xbuf[b][:, :], x[b * P:(b + 1) * P, :]).then_inc(x_in[b], 16)
                with sp.Fori(1, IMG_TILES // XB) as g:
                    for b in range(XB):
                        sp.wait_ge(back_done, (g - 1) * XB + b + 1)
                        sp.dma_start(xbuf[b][:, :], x[bass.ds(g * (XB * P) + b * P, P), :]).then_inc(x_in[b], 16)

            @block.scalar
            def _(act):
                for c in range(XC):
                    src = ws_t[c * 32:(c + 1) * 32, :].unsqueeze(1).to_broadcast([32, 4, D])
                    act.dma_start(tokw[:, c, :], src).then_inc(tokw_in, 16)
                act.dma_start(tokd[:, :], w_t.unsqueeze(0).to_broadcast([32, 4, D])).then_inc(tokw_in, 16)
                full = TILES - 1 - IMG_TILES
                act.wait_ge(txt_zero, 1)
                act.dma_start(h_all[:, IMG_TILES:TILES - 1, :],
                              txt[0:full * P, :].rearrange("(n p) f -> p n f", p=P)).then_inc(txt_in, 16)
                act.dma_start(h_all[0:TAIL, TILES - 1, :], txt[full * P:full * P + TAIL, :]).then_inc(txt_in, 16)
                for dst, src in (
                    (inw[:, :, :], in_w.rearrange("(c p) n -> p c n", p=P)),
                    (outw[:, :, :], out_w.rearrange("(c p) n -> p c n", p=P)),
                    (headw[:, :], head),
                    (ls[:, :], logit.unsqueeze(0).to_broadcast([P, H])),
                    (wq_s[:, :, :], wq.rearrange("(c p) n -> p c n", p=P)),
                    (wd_s[:, :, :], wd.rearrange("(c p) n -> p c n", p=P)),
                    (wu_s[0:LAT, :], wu),
                    (wu_s[LAT:LAT + 1, :], bu.unsqueeze(0)),
                    (wo_s[:, :, :], wo.rearrange("(c p) n -> p c n", p=P)),
                    (wg_s[:, :, :], wg.rearrange("(c p) n -> p c n", p=P)),
                    (we_s[:, 0, :, :], we[:, 0:P, :].rearrange("e p f -> p e f")),
                    (we_s[:, 1, :, :], we[:, P:D, :].rearrange("e p f -> p e f")),
                    (g1_s[:, :], g1),
                    (g2_s[:, :], g2),
                    (bd_s[:, :], bd.unsqueeze(1)),
                    (bias_f[:, 0:3 * D], in_b.unsqueeze(0).to_broadcast([3, 3 * D])),
                    (bias_f[:, 3 * D:4 * D], out_b.unsqueeze(0).to_broadcast([3, D])),
                    (bias_f[:, 4 * D:5 * D], bq.unsqueeze(0).to_broadcast([3, D])),
                    (bias_f[:, 5 * D:6 * D], bo.unsqueeze(0).to_broadcast([3, D])),
                    (bias_f[:, 6 * D:6 * D + E], bg.unsqueeze(0).to_broadcast([3, E])),
                    (pick[:, :], pick_c),
                    (am_f[:, :], amask_c),
                    (fm_f[:, :], fmask_c),
                ):
                    act.dma_start(dst, src).then_inc(w_in, 16)

                def front(i, p):
                    act.wait_ge(front_done, i + 1)
                    wait(act, mix_done, i - 1)
                    nc.scalar.activation(x_t[p][:, 0:4, :], bank[2 * p][:, :], ACT.Copy).then_inc(front_ready, 1)

                for b in range(XB):
                    front(b, b % 2)
                with act.Fori(1, IMG_TILES // XB) as g:
                    for b in range(XB):
                        front(g * XB + b, b % 2)

            @block.gpsimd
            def _(pool):
                nc.gpsimd.memset(h_all[96:128, TILES - 1, :], 0.0).then_inc(txt_zero, 1)
                pool.wait_ge(txt_zero, 1)
                nc.gpsimd.memset(neghalf[:, :], -0.5)
                nc.gpsimd.memset(ln_eps[:, :], LN_EPS)
                nc.gpsimd.memset(rms_eps[:, :], RMS_EPS)
                nc.gpsimd.memset(ones3[:, :], 1.0)
                nc.gpsimd.memset(kpad[:, :, :, :], 0.0)
                nc.gpsimd.memset(vaug[:, :, HD:HD + 1], 1.0)
                nc.gpsimd.memset(qpad[:, :, :], 0.0)
                nc.gpsimd.memset(v48[:, :, 33:48], 0.0)
                nc.gpsimd.memset(v48[:, :, 32:33], 1.0).then_inc(consts_ready, 1)
                pool.wait_ge(consts_ready, 1)
                nc.gpsimd.memset(lat[LAT:LAT + 1, :], 1.0).then_inc(consts_ready, 1)
                pool.wait_ge(consts_ready, 2)
                pool.wait_ge(w_in, 16 * 23)
                for c in range(KC):
                    for w, g in ((wq_s[:, c, :], g1_s), (wd_s[:, c, :], g1_s), (outw[:, c, :], headw),
                                 (wg_s[:, c, :], g2_s), (we_s[:, c, :, :], g2_s)):
                        nc.gpsimd.tensor_scalar(w, w, g[:, c:c + 1], 1.0, ALU.mult, ALU.mult)
                nc.gpsimd.tensor_copy(am[:, :], am_f[:, :])
                nc.gpsimd.tensor_copy(fm[:, :], fm_f[:, :]).then_inc(consts_ready, 1)

                with pool.Fori(0, TILES) as i:
                    pool.wait_ge(stats_ready, i + 1)
                    nc.gpsimd.tensor_tensor(vtmp[:, :], mv[:, 1:2], ln_eps[:, :], ALU.add)
                    nc.gpsimd.tensor_copy(cf[:, MEAN:MEAN + 1], mv[:, 0:1]).then_inc(c_var, 1)
                    settle(pool, consts_ready)
                    pool.wait_ge(c_var, i + 1)
                    nc.gpsimd.tensor_tensor(cf[:, RS:RS + 1], vtmp[:, :], neghalf[:, :], ALU.pow).then_inc(c_rs, 1)
                    settle(pool, consts_ready)
                    pool.wait_ge(c_rs, i + 1)
                    nc.gpsimd.tensor_copy(cf_all[:, bass.ds(i, 1), 0:2], cf[:, 0:2].unsqueeze(1)).then_inc(c_all, 1)
                    pool.wait_ge(c_all, i + 1)

            @block.vector
            def _(dve):
                dve.wait_ge(tokw_in, 16 * (XC + 1))
                nc.vector.tensor_tensor(tokw[:, :, :], tokw[:, :, :],
                                        tokd[:, :].unsqueeze(1).to_broadcast([P, XC, D]),
                                        ALU.mult).then_inc(tokw_ready, 1)

                def back(i, p):
                    dve.wait_ge(back_done, i + 1)
                    wait(dve, mix_done, i - 1)
                    nc.vector.tensor_copy(x_t[p][:, 4:8, :], bank[2 * p + 1][:, :]).then_inc(back_ready, 1)

                def take(i, p):
                    dve.wait_ge(mix_done, i + 1)
                    wait(dve, stats_ready, i)
                    wait(dve, c_var, i)
                    nc.vector.tensor_copy(h_all[:, bass.ds(i, 1), :], bank[4 + p][:, 0:D])
                    nc.vector.bn_stats(st[:, :], bank[4 + p][:, 0:D]).then_inc(h_ready, 1)
                    settle(dve, tokw_ready)
                    dve.wait_ge(h_ready, i + 1)
                    nc.vector.bn_aggr(mv[:, :], st[:, :]).then_inc(stats_ready, 1)

                for b in range(XB):
                    back(b, b % 2)
                    if b:
                        take(b - 1, (b - 1) % 2)
                with dve.Fori(1, IMG_TILES // XB) as g:
                    for b in range(XB):
                        back(g * XB + b, b % 2)
                        take(g * XB + b - 1, (b - 1) % 2)
                take(IMG_TILES - 1, (IMG_TILES - 1) % 2)
                dve.wait_ge(txt_in, 32)
                for i in range(IMG_TILES, TILES):
                    dve.wait_ge(c_var, i)
                    nc.vector.bn_stats(st[:, :], h_all[:, i, :]).then_inc(h_ready, 1)
                    dve.wait_ge(h_ready, i + 1)
                    nc.vector.bn_aggr(mv[:, :], st[:, :]).then_inc(stats_ready, 1)
                dve.wait_ge(w_in, 16 * 23)
                n = 0

                def linked(op):
                    nonlocal n
                    n += 1
                    op.then_inc(link1, 1)
                    dve.wait_ge(link1, n)

                left = bias_f
                for k in range(3):
                    linked(nc.vector.tensor_copy(bias_p[:, :], left[:, :]))
                    if k < 2:
                        linked(nc.vector.tensor_tensor(bias_l[:, :], left[:, :], bias_p[:, :], ALU.subtract))
                    if k == 0:
                        linked(nc.vector.tensor_scalar(bias_a[:, :], bias_p[:, :], pick[:, 0:1], None, ALU.mult))
                    else:
                        linked(nc.vector.scalar_tensor_tensor(out=bias_a[:, :], in0=bias_p[:, :], scalar=pick[:, k:k + 1],
                                                              in1=bias_a[:, :], op0=ALU.mult, op1=ALU.add))
                    left = bias_l
                nc.vector.tensor_copy(brow[:, :], bias_a[:, :])
                linked(nc.vector.tensor_scalar(ls[:, :], ls[:, :], 4.605170185988091, None, ALU.min))

            @block.tensor
            def _(pe):
                def turn(i, p, b, full):
                    pe.wait_ge(x_in[b], full)
                    for c in range(XC):
                        half = nc.tensor.transpose(bank[2 * p + c // 4][:, (c % 4) * P:(c % 4 + 1) * P],
                                                   xbuf[b][:, c * P:(c + 1) * P], ident[:, :])
                        if c == 3:
                            half.then_inc(front_done, 1)
                    half.then_inc(back_done, 1)

                def mix(i, p):
                    pe.wait_ge(front_ready, i + 1)
                    pe.wait_ge(back_ready, i + 1)
                    wait(pe, h_ready, i - 1)
                    for c in range(XC):
                        last = nc.tensor.matmul(bank[4 + p][:, 0:D], x_t[p][:, c, :], tokw[:, c, :],
                                                start=(c == 0), stop=(c == XC - 1))
                    last.then_inc(mix_done, 1)

                pe.wait_ge(c_in, 16)
                for b in range(XB):
                    turn(b, b % 2, b, 16)
                    if b == 1:
                        pe.wait_ge(tokw_ready, 1)
                    if b:
                        mix(b - 1, (b - 1) % 2)
                with pe.Fori(1, IMG_TILES // XB) as g:
                    for b in range(XB):
                        turn(g * XB + b, b % 2, b, g * 16 + 16)
                        mix(g * XB + b - 1, (b - 1) % 2)
                mix(IMG_TILES - 1, (IMG_TILES - 1) % 2)

        names = ("ls_ready", "a_xn", "a_xnps", "a_xnt", "a_qkv", "a_sq", "a_v", "a_ss", "a_rn", "a_qk", "a_qkt",
                 "a_s", "a_max", "a_sub", "a_exp", "a_prt", "a_av", "a_rsum", "a_on", "a_onps", "a_ont", "a_out",
                 "a_h", "a_st", "a_mv", "p_var", "p_rs", "p_ms", "p_mse", "p_rms", "p_rr", "p_h",
                 "p_all", "a_link")
        (ls_ready, a_xn, a_xnps, a_xnt, a_qkv, a_sq, a_v, a_ss, a_rn, a_qk, a_qkt, a_s, a_max, a_sub, a_exp, a_prt,
         a_av, a_rsum, a_on, a_onps, a_ont, a_out, a_h, a_st, a_mv, p_var, p_rs, p_ms, p_mse, p_rms, p_rr, p_h,
         p_all, a_link) = map(sem, names)
        b_xt, b_qk, b_v, b_s, b_o, b_ot, b_out = bank[0:7]

        with nc.Block() as block:
            @block.tensor
            def _(pe):
                def body(i):
                    if real(i, 0):
                        pe.wait_ge(a_qkt, i + 1)
                        nc.tensor.matmul(b_s[:, :], am[:, 0:P], am[:, P:], start=True, stop=True,
                                         skip_group_check=True)
                        for pair in range(8):
                            for j in range(4):
                                q = slice(32 * j, 32 * j + 32)
                                last = nc.tensor.matmul(b_s[q, pair * 64:pair * 64 + 64], q_t[q, pair, :], k_t[q, pair, :],
                                                        start=False, stop=True, skip_group_check=True)
                        last.then_inc(a_s, 1)
                    if real(i, -1):
                        pe.wait_ge(a_on, i)
                        for c in range(KC):
                            last = nc.tensor.transpose(b_ot[:, c * P:(c + 1) * P],
                                                       on[:, :, :].rearrange("p h d -> p (h d)")[:, c * P:(c + 1) * P],
                                                       ident[:, :])
                        last.then_inc(a_onps, 1)
                    if real(i, 1):
                        pe.wait_ge(a_xnt, i + 2)
                        wait(pe, a_qk, i + 1)
                        wait(pe, a_v, i + 1)
                        for half, (dst, n0, n1) in enumerate(((b_qk, 0, 2 * D), (b_v, 2 * D, 3 * D))):
                            for c in range(KC):
                                nc.tensor.matmul(dst[:, 0:n1 - n0], xn_t[:, c, :], inw[:, c, n0:n1],
                                                 start=(c == 0), stop=False)
                            last = nc.tensor.matmul(dst[:, 0:n1 - n0], ones3[:, :], brow[:, n0:n1], start=False, stop=True)
                        last.then_inc(a_qkv, 1)
                    if real(i, -1):
                        pe.wait_ge(a_ont, i)
                        wait(pe, a_h, i - 1)
                        for c in range(KC):
                            nc.tensor.matmul(b_out[:, 0:D], on_t[:, c, :], outw[:, c, :], start=(c == 0), stop=False)
                        nc.tensor.matmul(b_out[:, 0:D], ones3[:, :], brow[:, 3 * D:4 * D], start=False,
                                         stop=True).then_inc(a_out, 1)
                    if real(i, 0):
                        settle(pe, c_in)
                        pe.wait_ge(a_prt, i + 1)
                        pe.wait_ge(a_v, i + 1)
                        for h in range(H):
                            for j in range(4):
                                q = slice(32 * j, 32 * j + 32)
                                last = nc.tensor.matmul(b_o[q, h * 17:h * 17 + 17], pr_t[q, h, :], vaug[q, h, :],
                                                        start=True, stop=True)
                        last.then_inc(a_av, 1)
                    if real(i, 2):
                        pe.wait_ge(a_xn, i + 3)
                        for c in range(KC):
                            last = nc.tensor.transpose(b_xt[:, c * P:(c + 1) * P], xn[:, c * P:(c + 1) * P], ident[:, :])
                        last.then_inc(a_xnps, 1)

                tiles_in_order(pe, body, 1, 2)

            @block.scalar
            def _(act):
                nc.scalar.activation(ls[:, :], ls[:, :], ACT.Exp).then_inc(ls_ready, 1)

                def body(i):
                    if real(i, -1):
                        act.wait_ge(a_onps, i)
                        wait(act, a_out, i - 1)
                        nc.scalar.activation(on_t[:, :, :], b_ot[:, 0:D], ACT.Copy).then_inc(a_ont, 1)
                    if real(i, 0):
                        act.wait_ge(a_sub, i + 1)
                        nc.scalar.activation(pr[:, :, :], sc[:, :, :], ACT.Exp).then_inc(a_exp, 1)
                    if real(i, 1):
                        act.wait_ge(a_qkv, i + 2)
                        wait(act, a_ss, i + 1)
                        nc.scalar.activation(sq[:, :, :], b_qk[:, :], ACT.Square).then_inc(a_sq, 1)
                        wait(act, a_av, i + 1)
                        nc.scalar.activation(vaug[:, :, 0:HD], b_v[:, 0:D], ACT.Copy).then_inc(a_v, 1)
                    if real(i, 2):
                        act.wait_ge(a_xnps, i + 3)
                        wait(act, a_qkv, i + 2)
                        nc.scalar.activation(xn_t[:, :, :], b_xt[:, 0:D], ACT.Copy).then_inc(a_xnt, 1)

                tiles_in_order(act, body, 1, 2)

            @block.vector
            def _(dve):
                def link(i, k, op):
                    op.then_inc(a_link, 1)
                    dve.wait_ge(a_link, i * 12 + k + 1)

                def body(i):
                    if real(i, 0):
                        dve.wait_ge(a_s, i + 1)
                        s3 = b_s[:, :].rearrange("p (h m) -> p h m", h=H)
                        nc.vector.tensor_reduce(smax[:, :], s3, AX.X, ALU.max).then_inc(a_max, 1)
                        dve.wait_ge(a_max, i + 1)
                        wait(dve, a_exp, i)
                        nc.vector.tensor_tensor(sc[:, :, :], s3, smax[:, :].unsqueeze(2).to_broadcast([P, H, 32]),
                                                ALU.subtract).then_inc(a_sub, 1)
                    if real(i, 2):
                        wait(dve, a_xnps, i + 2)
                        m = cf_all[:, bass.ds(i + 2, 1), MEAN:MEAN + 1].squeeze(1)
                        r = cf_all[:, bass.ds(i + 2, 1), RS:RS + 1].squeeze(1)
                        nc.vector.tensor_scalar(xn[:, :], h_all[:, bass.ds(i + 2, 1), :].squeeze(1), m, r,
                                                ALU.subtract, ALU.mult).then_inc(a_xn, 1)
                    if real(i, 0):
                        dve.wait_ge(a_exp, i + 1)
                        wait(dve, a_av, i)
                        nc.vector.transpose(pr_t[:, :, :], pr[:, :, :]).then_inc(a_prt, 1)
                    if real(i, -1):
                        dve.wait_ge(a_out, i)
                        wait(dve, p_h, i - 1)
                        nc.vector.tensor_tensor(hnew[:, :], b_out[:, 0:D], h_all[:, bass.ds(i - 1, 1), :].squeeze(1),
                                                ALU.add).then_inc(a_h, 1)
                        dve.wait_ge(a_h, i)
                        nc.vector.bn_stats(st[:, :], hnew[:, :]).then_inc(a_st, 1)
                    if real(i, 1):
                        dve.wait_ge(a_sq, i + 2)
                        nc.vector.tensor_reduce(ss[:, :], sq[:, :, :], AX.X, ALU.add).then_inc(a_ss, 1)
                    if real(i, -1):
                        settle(dve, tokw_ready)
                        dve.wait_ge(a_st, i)
                        wait(dve, p_ms, i - 1)
                        nc.vector.bn_aggr(mv[:, :], st[:, :]).then_inc(a_mv, 1)
                    if real(i, 1):
                        dve.wait_ge(a_ss, i + 2)
                        t = i + 1
                        link(t, 0, nc.vector.tensor_scalar(ss[:, :], ss[:, :], 1e-24, None, ALU.max))
                        link(t, 1, nc.vector.tensor_scalar(guess[:, :].bitcast(U32), ss[:, :].bitcast(U32), 1, None,
                                                           ALU.logical_shift_right))
                        link(t, 2, nc.vector.tensor_scalar(rn[:, :].bitcast(I32), guess[:, :].bitcast(I32), -1.0,
                                                           float(RSQRT_MAGIC), ALU.mult, ALU.add))
                        for k in range(3):
                            link(t, 3 + 3 * k, nc.vector.tensor_tensor(rt[:, :], rn[:, :], rn[:, :], ALU.mult))
                            link(t, 4 + 3 * k, nc.vector.scalar_tensor_tensor(out=rt[:, :], in0=rt[:, :], scalar=-0.5,
                                                                              in1=ss[:, :], op0=ALU.mult, op1=ALU.mult))
                            link(t, 5 + 3 * k, nc.vector.scalar_tensor_tensor(out=rn[:, :], in0=rt[:, :], scalar=1.5,
                                                                              in1=rn[:, :], op0=ALU.add, op1=ALU.mult))
                        if isinstance(i, int) and i == -1:
                            dve.wait_ge(ls_ready, 1)
                        nc.vector.tensor_tensor(rn[:, 0:H], rn[:, 0:H], ls[:, :], ALU.mult).then_inc(a_rn, 1)
                        nc.vector.tensor_tensor(kpad[:, :, 0:4:3, :], b_qk[:, D:2 * D].rearrange("p (a s d) -> p a s d", s=2, d=HD),
                                                rn[:, H:].rearrange("p (a s) -> p a s", s=2).unsqueeze(3).to_broadcast([P, 8, 2, HD]),
                                                ALU.mult)
                        dve.wait_ge(a_rn, i + 2)
                        nc.vector.tensor_tensor(qn[:, :, :], b_qk[:, 0:D].rearrange("p (h d) -> p h d", d=HD),
                                                rn[:, 0:H].unsqueeze(2).to_broadcast([P, H, HD]),
                                                ALU.mult).then_inc(a_qk, 1)
                        dve.wait_ge(a_qk, i + 2)
                        nc.vector.transpose(k_t[:, :, :], kpad[:, :, :, :])
                        nc.vector.transpose(q_t[:, :, :], qn[:, :, :]).then_inc(a_qkt, 1)
                    if real(i, 0):
                        dve.wait_ge(a_av, i + 1)
                        o3 = b_o[:, 0:H * 17].rearrange("p (h d) -> p h d", d=17)
                        nc.vector.reciprocal(rsum[:, :], o3[:, :, HD:HD + 1]).then_inc(a_rsum, 1)
                        dve.wait_ge(a_rsum, i + 1)
                        wait(dve, a_onps, i)
                        nc.vector.tensor_tensor(on[:, :, :], o3[:, :, 0:HD], rsum[:, :].unsqueeze(2).to_broadcast([P, H, HD]),
                                                ALU.mult).then_inc(a_on, 1)

                tiles_in_order(dve, body, 1, 2)

            @block.gpsimd
            def _(pool):
                with pool.Fori(0, TILES) as i:
                    settle(pool, consts_ready)
                    pool.wait_ge(a_h, i + 1)
                    nc.gpsimd.tensor_copy(h_all[:, bass.ds(i, 1), :], hnew[:, :].unsqueeze(1)).then_inc(p_h, 1)
                    settle(pool, consts_ready)
                    pool.wait_ge(a_mv, i + 1)
                    nc.gpsimd.tensor_tensor(vtmp[:, :], mv[:, 1:2], ln_eps[:, :], ALU.add).then_inc(p_var, 1)
                    settle(pool, consts_ready)
                    pool.wait_ge(p_var, i + 1)
                    nc.gpsimd.tensor_tensor(cf[:, RS:RS + 1], vtmp[:, :], neghalf[:, :], ALU.pow).then_inc(p_rs, 1)
                    settle(pool, consts_ready)
                    pool.wait_ge(p_rs, i + 1)
                    nc.gpsimd.tensor_scalar(ms[:, :], mv[:, 1:2], cf[:, RS:RS + 1], cf[:, RS:RS + 1], ALU.mult, ALU.mult)
                    nc.gpsimd.tensor_copy(cf[:, MEAN:MEAN + 1], mv[:, 0:1])
                    nc.gpsimd.tensor_scalar(cf[:, NM:NM + 1], mv[:, 0:1], cf[:, RS:RS + 1], -1.0, ALU.mult,
                                            ALU.mult).then_inc(p_ms, 1)
                    settle(pool, consts_ready)
                    pool.wait_ge(p_ms, i + 1)
                    nc.gpsimd.tensor_scalar(mse[:, :], ms[:, :], 1.0, RMS_EPS, ALU.mult, ALU.add).then_inc(p_mse, 1)
                    settle(pool, consts_ready)
                    pool.wait_ge(p_mse, i + 1)
                    nc.gpsimd.tensor_tensor(ms2[:, :], mse[:, :], neghalf[:, :], ALU.pow).then_inc(p_rms, 1)
                    settle(pool, consts_ready)
                    pool.wait_ge(p_rms, i + 1)
                    nc.gpsimd.tensor_tensor(cf[:, RR:RR + 1], ms2[:, :], cf[:, RS:RS + 1], ALU.mult).then_inc(p_rr, 1)
                    settle(pool, consts_ready)
                    pool.wait_ge(p_rr, i + 1)
                    nc.gpsimd.tensor_copy(cf_all[:, bass.ds(i, 1), :], cf[:, :].unsqueeze(1)).then_inc(p_all, 1)
                    pool.wait_ge(p_all, i + 1)

        names = ("f_hn", "f_hnps", "f_hnt", "f_q", "f_down", "f_lat", "f_qpad", "f_kv", "f_kvt", "f_qt", "f_v", "f_s", "f_max",
                 "f_sub", "f_exp", "f_prt", "f_av", "f_of", "f_rsum", "f_on", "f_onps", "f_ont", "f_wo", "f_x2",
                 "f_ss2", "f_h2", "f_h2ps", "f_h2t", "f_gate", "f_gmax", "f_gexp", "f_grec", "f_gmul", "f_we",
                 "f_comb", "f_acc", "f_x1", "p_hx2", "p_t2", "p_r2", "out_done")
        (f_hn, f_hnps, f_hnt, f_q, f_down, f_lat, f_qpad, f_kv, f_kvt, f_qt, f_v, f_s, f_max,
         f_sub, f_exp, f_prt, f_av, f_of, f_rsum, f_on, f_onps, f_ont, f_wo, f_x2,
         f_ss2, f_h2, f_h2ps, f_h2t, f_gate, f_gmax, f_gexp, f_grec, f_gmul, f_we,
         f_comb, f_acc, f_x1, p_hx2, p_t2, p_r2, out_done) = map(sem, names)
        b_we, b_s, b_o, b_kv, b_turn, b_q, b_hn = bank[0:2], bank[2], bank[3], bank[4], bank[5], bank[6], bank[7]
        b_down, b_gate, b_wo = b_turn[0:LAT, D:D + P], b_q[:, D:D + E], b_hn[:, 0:D]
        EP = 2
        STEPS = E // EP

        with nc.Block() as block:
            @block.tensor
            def _(pe):
                def body(i):
                    if real(i, 0):
                        pe.wait_ge(f_qt, i + 1)
                        nc.tensor.matmul(b_s[:, :], fm[:, 0:P], fm[:, P:], start=True, stop=True,
                                         skip_group_check=True)
                        for pair in range(16):
                            for j in range(4):
                                q = slice(32 * j, 32 * j + 32)
                                last = nc.tensor.matmul(b_s[q, pair * 32:pair * 32 + 32], fq_t[q, 2 * pair:2 * pair + 2, :].rearrange("r t h -> r (t h)"),
                                                        kv_t[q, :, 2 * pair:2 * pair + 2],
                                                        start=False, stop=True, skip_group_check=True)
                        last.then_inc(f_s, 1)
                    if real(i, -1):
                        pe.wait_ge(f_on, i)
                        wait(pe, f_h2t, i - 1)
                        for c in range(KC):
                            last = nc.tensor.transpose(b_turn[:, c * P:(c + 1) * P],
                                                       on[:, :, :].rearrange("p h d -> p (h d)")[:, c * P:(c + 1) * P],
                                                       ident[:, :])
                        last.then_inc(f_onps, 1)
                    if real(i, 1):
                        pe.wait_ge(f_hnt, i + 2)
                        wait(pe, f_gexp, i - 1)
                        for c in range(KC):
                            nc.tensor.matmul(b_q[:, 0:D], hn_t[:, c, :], wq_s[:, c, :], start=(c == 0), stop=False)
                        nc.tensor.matmul(b_q[:, 0:D], ones3[:, :], brow[:, 4 * D:5 * D], start=False,
                                         stop=True).then_inc(f_q, 1)
                        wait(pe, f_ont, i)
                        for c in range(KC):
                            last = nc.tensor.matmul(b_down, wd_s[:, c, :], hn_t[:, c, :], start=(c == 0),
                                                    stop=(c == KC - 1))
                        last.then_inc(f_down, 1)
                    if real(i, -1):
                        pe.wait_ge(f_ont, i)
                        for c in range(KC):
                            nc.tensor.matmul(b_wo, on_t[:, c, :], wo_s[:, c, :], start=(c == 0), stop=False)
                        nc.tensor.matmul(b_wo, ones3[:, :], brow[:, 5 * D:6 * D], start=False,
                                         stop=True).then_inc(f_wo, 1)
                    if real(i, 1):
                        pe.wait_ge(f_lat, i + 2)
                        wait(pe, f_kvt, i + 1)
                        nc.tensor.matmul(b_kv[:, :], lat[:, :], wu_s[:, :], start=True, stop=True).then_inc(f_kv, 1)
                    if real(i, 0):
                        settle(pe, c_in)
                        pe.wait_ge(f_prt, i + 1)
                        pe.wait_ge(f_v, i + 1)
                        wait(pe, f_of, i)
                        for pair in range(16):
                            for j in range(4):
                                q = slice(32 * j, 32 * j + 32)
                                last = nc.tensor.matmul(b_o[q, pair * 32:pair * 32 + 32], v48[q, pair, 16:48], pr_t[q, pair, :],
                                                        start=True, stop=True)
                        last.then_inc(f_av, 1)
                    if real(i, -1):
                        pe.wait_ge(f_h2, i)
                        for c in range(KC):
                            last = nc.tensor.transpose(b_turn[:, c * P:(c + 1) * P], h2[:, c * P:(c + 1) * P], ident[:, :])
                        last.then_inc(f_h2ps, 1)
                    if real(i, 2):
                        pe.wait_ge(f_hn, i + 3)
                        wait(pe, f_x2, i)
                        for c in range(KC):
                            last = nc.tensor.transpose(b_hn[:, c * P:(c + 1) * P], hn[:, c * P:(c + 1) * P], ident[:, :])
                        last.then_inc(f_hnps, 1)
                    if real(i, -1):
                        pe.wait_ge(f_h2t, i)
                        if real(i, 1):
                            pe.wait_ge(f_qpad, i + 2)
                        for c in range(KC):
                            nc.tensor.matmul(b_gate, h2_t[:, c, :], wg_s[:, c, :], start=(c == 0), stop=False)
                        nc.tensor.matmul(b_gate, ones3[:, :], brow[:, 6 * D:6 * D + E], start=False,
                                         stop=True).then_inc(f_gate, 1)
                        for s in range(STEPS):
                            wait(pe, f_comb, (i - 1) * STEPS + s - 1)
                            for c in range(KC):
                                last = nc.tensor.matmul(b_we[s % 2][:, :], h2_t[:, c, :],
                                                        we_s[:, c, s * EP:(s + 1) * EP, :], start=(c == 0), stop=(c == KC - 1))
                            last.then_inc(f_we, 1)

                tiles_in_order(pe, body, 1, 2)

            @block.scalar
            def _(act):
                def body(i):
                    if real(i, -1):
                        act.wait_ge(f_onps, i)
                        wait(act, f_wo, i - 1)
                        nc.scalar.activation(on_t[:, :, :], b_turn[:, 0:D], ACT.Copy).then_inc(f_ont, 1)
                    if real(i, 1):
                        act.wait_ge(f_down, i + 2)
                        wait(act, f_kv, i + 1)
                        nc.scalar.activation(lat[0:LAT, :], b_down, ACT.Identity, bias=bd_s[:, :]).then_inc(f_lat, 1)
                    if real(i, 0):
                        act.wait_ge(f_sub, i + 1)
                        wait(act, f_prt, i)
                        nc.scalar.activation(pr[:, :, :], sc[:, :, :], ACT.Exp, scale=HD ** -0.5).then_inc(f_exp, 1)
                    if real(i, -1):
                        act.wait_ge(f_x2, i)
                        wait(act, p_t2, i - 1)
                        nc.scalar.activation(junk[:, :], x2[:, :], ACT.Square, scale=D ** -0.5,
                                             accum_out=ss2[:, :]).then_inc(f_ss2, 1)
                        act.wait_ge(f_h2ps, i)
                        wait(act, f_we, (i - 1) * STEPS)
                        nc.scalar.activation(h2_t[:, :, :], b_turn[:, 0:D], ACT.Copy).then_inc(f_h2t, 1)
                    if real(i, 2):
                        act.wait_ge(f_hnps, i + 3)
                        wait(act, f_down, i + 2)
                        nc.scalar.activation(hn_t[:, :, :], b_hn[:, 0:D], ACT.Copy).then_inc(f_hnt, 1)
                    if real(i, -1):
                        act.wait_ge(f_gmax, i)
                        wait(act, f_gmul, i - 1)
                        nc.scalar.activation(gexp[:, :], b_gate, ACT.Exp, bias=gmax[:, :],
                                             accum_out=gsum[:, :]).then_inc(f_gexp, 1)

                    if real(i, 0):
                        settle(act, ls_ready)
                        wait(act, f_x2, i)
                        at = bass.ds(i, 1)
                        nc.scalar.activation(x1[:, :], h_all[:, at, :].squeeze(1), ACT.Identity,
                                             bias=cf_all[:, at, NM:NM + 1].squeeze(1),
                                             scale=cf_all[:, at, RS:RS + 1].squeeze(1)).then_inc(f_x1, 1)

                tiles_in_order(act, body, 1, 2)

            @block.vector
            def _(dve):
                def body(i):
                    if real(i, 0):
                        dve.wait_ge(f_s, i + 1)
                        s3 = b_s[:, :].rearrange("p (h m) -> p h m", m=32)
                        nc.vector.tensor_reduce(smax[:, :], s3, AX.X, ALU.max).then_inc(f_max, 1)
                        dve.wait_ge(f_max, i + 1)
                        wait(dve, f_exp, i)
                        nc.vector.tensor_tensor(sc[:, :, :], s3, smax[:, :].unsqueeze(2).to_broadcast([P, 16, 32]),
                                                ALU.subtract).then_inc(f_sub, 1)
                    if real(i, 1):
                        dve.wait_ge(f_q, i + 2)
                        nc.vector.tensor_copy(qpad[:, :, 0:HD], b_q[:, 0:D].rearrange("p (h d) -> p h d", d=HD)).then_inc(f_qpad, 1)
                    if real(i, 2):
                        wait(dve, f_hnps, i + 2)
                        at = bass.ds(i + 2, 1)
                        nc.vector.tensor_scalar(hn[:, :], h_all[:, at, :].squeeze(1), cf_all[:, at, MEAN:MEAN + 1].squeeze(1),
                                                cf_all[:, at, RR:RR + 1].squeeze(1), ALU.subtract, ALU.mult).then_inc(f_hn, 1)
                    if real(i, 0):
                        dve.wait_ge(f_exp, i + 1)
                        wait(dve, f_av, i)
                        nc.vector.transpose(pr_t[:, :, :], pr[:, :, :]).then_inc(f_prt, 1)
                    if real(i, -1):
                        dve.wait_ge(f_wo, i)
                        dve.wait_ge(f_x1, i)
                        wait(dve, p_hx2, i - 1)
                        wait(dve, f_ss2, i - 1)
                        nc.vector.tensor_tensor(x2[:, :], b_wo, x1[:, :], ALU.add).then_inc(f_x2, 1)
                    if real(i, 1):
                        dve.wait_ge(f_kv, i + 2)
                        nc.vector.transpose(kv_t[:, :, :], b_kv[:, :]).then_inc(f_kvt, 1)
                        dve.wait_ge(f_qpad, i + 2)
                        nc.vector.transpose(fq_t[:, :, :].rearrange("r t h -> r h t"), qpad[:, :, :]).then_inc(f_qt, 1)
                    if real(i, -1):
                        dve.wait_ge(p_r2, i)
                        wait(dve, f_h2ps, i - 1)
                        nc.vector.tensor_scalar(h2[:, :], x2[:, :], r2[:, :], None, ALU.mult).then_inc(f_h2, 1)
                    if real(i, 0):
                        dve.wait_ge(f_av, i + 1)
                        nc.vector.transpose(of[:, :, :], b_o[:, :].rearrange("r (t h) -> r h t", h=H)).then_inc(f_of, 1)
                        dve.wait_ge(f_of, i + 1)
                        nc.vector.reciprocal(rsum[:, :], of[:, :, HD:HD + 1]).then_inc(f_rsum, 1)
                        dve.wait_ge(f_rsum, i + 1)
                        wait(dve, f_onps, i)
                        nc.vector.tensor_tensor(on[:, :, :], of[:, :, 0:HD], rsum[:, :].unsqueeze(2).to_broadcast([P, H, HD]),
                                                ALU.mult).then_inc(f_on, 1)
                    if real(i, -1):
                        dve.wait_ge(f_gate, i)
                        nc.vector.tensor_reduce(gmax[:, :], b_gate, AX.X, ALU.max, negate=True).then_inc(f_gmax, 1)
                    if real(i, 1):
                        dve.wait_ge(f_kvt, i + 2)
                        nc.vector.transpose(v48[:, :, 0:32],
                                            kv_t[:, :, :].rearrange("r g (p t) -> r p g t", t=2)).then_inc(f_v, 1)
                    if real(i, -1):
                        dve.wait_ge(f_gexp, i)
                        nc.vector.reciprocal(grec[:, :], gsum[:, :]).then_inc(f_grec, 1)
                        dve.wait_ge(f_grec, i)
                        nc.vector.tensor_scalar(gate[:, :], gexp[:, :], grec[:, :], None, ALU.mult).then_inc(f_gmul, 1)
                        dve.wait_ge(f_gmul, i)
                        dve.wait_ge(p_hx2, i)
                        for e in range(E):
                            s, k = e // EP, e % EP
                            if k == 0:
                                dve.wait_ge(f_we, (i - 1) * STEPS + s + 1)
                            if e:
                                dve.wait_ge(f_acc if k else f_comb, (i - 1) * STEPS + (s + 1 if k else s))
                            if e == E - 1:
                                wait(dve, out_done, (i - 1) * 16)
                            op = nc.vector.scalar_tensor_tensor(
                                out=(res if e == E - 1 else acc)[:, :], in0=b_we[s % 2][:, k * D:(k + 1) * D],
                                scalar=gate[:, e:e + 1], in1=(acc if e else hx2)[:, :], op0=ALU.mult, op1=ALU.add)
                            op.then_inc(f_comb if k else f_acc, 1)

                tiles_in_order(dve, body, 1, 2)

            @block.gpsimd
            def _(pool):
                def body(i):
                    at = bass.ds(i, 1)
                    hi = h_all[:, at, :].squeeze(1)
                    pool.wait_ge(f_ss2, i + 1)
                    nc.gpsimd.tensor_tensor(t2[:, :], ss2[:, :], rms_eps[:, :], ALU.add).then_inc(p_t2, 1)
                    settle(pool, consts_ready)
                    pool.wait_ge(p_t2, i + 1)
                    wait(pool, f_h2, i)
                    nc.gpsimd.tensor_tensor(r2[:, :], t2[:, :], neghalf[:, :], ALU.pow).then_inc(p_r2, 1)
                    settle(pool, consts_ready)
                    wait(pool, f_comb, (i - 1) * STEPS + 1)
                    nc.gpsimd.tensor_tensor(hx2[:, :], hi, x2[:, :], ALU.add).then_inc(p_hx2, 1)

                body(0)
                body(1)
                with pool.Fori(2, TILES) as i:
                    body(i)

            @block.sync
            def _(sp):
                with sp.Fori(0, TILES - 1) as i:
                    sp.wait_ge(f_comb, (i + 1) * STEPS)
                    sp.dma_start(out[bass.ds(i * P, P), :], res[:, :]).then_inc(out_done, 16)
                sp.wait_ge(f_comb, TILES * STEPS)
                sp.dma_start(out[(TILES - 1) * P:TOKENS, :], res[0:TAIL, :]).then_inc(out_done, 16)
                sp.wait_ge(out_done, TILES * 16)


def kernel(**inputs):
    import numpy as np
    import concourse.bacc as bacc
    from concourse.bass_utils import run_bass_kernel_spmd

    a = {n: np.asarray(v) for n, v in inputs.items()}

    def rows(t):
        return np.ascontiguousarray(np.swapaxes(t, 0, 1)).reshape(t.shape[0] * t.shape[1], -1)

    def columns(v):
        return v.reshape(KC, P).T

    p, c = np.arange(P), np.arange(512)

    def mask(group, of_row, of_column):
        k = np.arange(group)[:, None]
        return np.concatenate([(of_row(p) == k), (of_column(c) != k) * -BIG], axis=1).astype(np.float32)

    arrays = {
        "x": rows(a["x"].reshape(B, N_IMG, FX)), "txt": rows(a["txt"]),
        "ws_t": a["L0_tok_weighted_sum"].T, "w_t": a["L0_tok_weight"].T,
        "in_w": a["L0_attn_in_proj_weight"].T, "in_b": a["L0_attn_in_proj_bias"],
        "logit": a["L0_attn_logit_scale"].reshape(H),
        "head": columns(np.repeat(a["L0_attn_head_scale"].reshape(H), HD)),
        "out_w": a["L0_attn_out_w"].T, "out_b": a["L0_attn_out_b"],
        "g1": columns(a["L0_ffn_gamma1"]), "wq": a["L0_ffn_Wq"], "bq": a["L0_ffn_bq"],
        "wd": a["L0_ffn_Wdown"], "bd": a["L0_ffn_bdown"], "wu": a["L0_ffn_Wup"], "bu": a["L0_ffn_bup"],
        "wo": a["L0_ffn_Wo"], "bo": a["L0_ffn_bo"], "g2": columns(a["L0_ffn_gamma2"]),
        "wg": a["L0_ffn_Wg"], "bg": a["L0_ffn_bg"], "we": a["L0_ffn_We"],
        "ident_c": np.eye(P, dtype=np.float32),
        "amask_c": mask(4, lambda n: n % 32 // B, lambda n: n % 32 // B), "fmask_c": mask(2, lambda n: n % 32 // 16, lambda n: n % 2),
        "pick_c": np.eye(3, dtype=np.float32),
    }
    nc = bacc.Bacc("TRN2", target_bir_lowering=False, num_devices=1)
    put, args = {}, {}
    for name, v in arrays.items():
        put[f"in_{name}"] = np.ascontiguousarray(v)
        args[name] = nc.dram_tensor(f"in_{name}", v.shape, mybir.dt.from_np(v.dtype), kind="ExternalInput").ap()
    out = nc.dram_tensor("out", (TOKENS, D), F32, kind="ExternalOutput").ap()
    build(nc, out=out, **args)
    r = run_bass_kernel_spmd(nc, [put], core_ids=[0])
    got = r.results[0]["out"].reshape(N_IMG + N_TXT, B, D)
    return np.ascontiguousarray(np.swapaxes(got, 0, 1))
```

```python
import concourse.bass as bass
from concourse import mybir
from contextlib import ExitStack

F32 = mybir.dt.float32
BF16 = mybir.dt.bfloat16
F16 = mybir.dt.float16
U32 = mybir.dt.uint32
I32 = mybir.dt.int32
ALU = mybir.AluOpType
ACT = mybir.ActivationFunctionType
AX = mybir.AxisListType

P = 128
B = 8
N_IMG, N_TXT = 512, 77
D = 256
KC = D // P
H, HD = 16, 16
FX = D * 4
XC = FX // P
IMG_TILES = N_IMG * B // P
TOKENS = (N_IMG + N_TXT) * B
TILES = -(-TOKENS // P)
TAIL = TOKENS - (TILES - 1) * P
LAT = 64
E = 8
BIG = float(2 ** 120)
RSQRT_MAGIC = 0x5F3759DF
LN_EPS, RMS_EPS = 1e-5, 1e-6
MEAN, RS, NM, RR = range(4)
XB = 4
WS = 256.0
NBIAS = 3 * D + D + D + D + E




def wait(eng, sem, value):
    if not isinstance(value, int) or value > 0:
        eng.wait_ge(sem, value)


def settle(eng, sem):
    eng.wait_ge(sem, 1)


def tiles_in_order(eng, body, back, ahead):
    first = (back + 3) // 2 * 2
    turns = (TILES - ahead - first) // 2
    for i in range(-ahead, first):
        body(i, i % 2)
    with eng.Fori(first // 2, first // 2 + turns) as g:
        for p in range(2):
            body(g * 2 + p, p)
    for i in range(first + 2 * turns, TILES + back):
        body(i, i % 2)


def real(i, k):
    return not isinstance(i, int) or 0 <= i + k < TILES


def build(nc, x, txt, ws_t, w_t, in_w, in_b, logit, head, out_w, out_b, g1, wq, bq, wd, bd, wu, bu,
          wo, bo, g2, wg, bg, we, ident_c, amask_c, fmask_c, pick_c, out):
    with ExitStack() as ctx, ExitStack() as phase1:
        def sb(name, shape, dt=F32, stack=ctx):
            return stack.enter_context(nc.sbuf_tensor(name, shape, dt))

        def halves(name, shape):
            return sb(name + "_h", shape, F16), sb(name + "_l", shape, F16)

        def sem(name):
            return ctx.enter_context(nc.semaphore(name))

        h_all = sb("h_all", [P, TILES, D])
        cf_all = sb("cf_all", [P, TILES, 4])
        ident = sb("ident", [P, P])
        inw_h, inw_l = halves("inw", [P, KC, 3 * D])
        outw_h, outw_l = halves("outw", [P, KC, D])
        wq_h, wq_l = halves("wq", [P, KC, D])
        wd_h, wd_l = halves("wd", [P, KC, LAT])
        wu_s = sb("wu_s", [LAT + 1, 2 * D])
        wo_h, wo_l = halves("wo", [P, KC, D])
        wg_h, wg_l = halves("wg", [P, KC, E])
        we_h, we_l = halves("we", [P, KC, E, D])
        ls = sb("ls", [P, H])
        bd_s = sb("bd_s", [LAT, 1])
        brow = sb("brow", [3, NBIAS], BF16)
        ones3 = sb("ones3", [3, P], BF16)
        am = sb("am", [4, P + 512], BF16)
        fm = sb("fm", [2, P + 512], BF16)
        neghalf = sb("neghalf", [P, TILES])
        onehalf = sb("onehalf", [P, 2 * H])
        ln_eps = sb("ln_eps", [P, 1])
        rms_eps = sb("rms_eps", [P, 1])
        st = sb("st", [P, 6])
        mv = sb("mv", [P, 2])
        kpad = sb("kpad", [P, H // 2, 4, HD])
        vaug = [sb(f"vaug{p}", [P, H, HD + 1]) for p in range(2)]
        lat = sb("lat", [LAT + 1, P])
        qpad = sb("qpad", [P, H, 32])
        v48 = [sb(f"v48_{p}", [P, 16, 48]) for p in range(2)]

        def sb1(name, shape, dt=F32):
            return sb(name, shape, dt, phase1)

        def halves1(name, shape):
            return sb1(name + "_h", shape, F16), sb1(name + "_l", shape, F16)

        tokw = sb1("tokw", [P, XC, D])
        tokw_h, tokw_l = halves1("tokw", [P, XC, D])
        tokd = sb1("tokd", [P, D])
        inw = sb1("inw", [P, KC, 3 * D])
        outw = sb1("outw", [P, KC, D])
        headw = sb1("headw", [P, KC])
        wq_s = sb1("wq_s", [P, KC, D])
        wd_s = sb1("wd_s", [P, KC, LAT])
        wo_s = sb1("wo_s", [P, KC, D])
        wg_s = sb1("wg_s", [P, KC, E])
        we_s = sb1("we_s", [P, KC, E, D])
        g1_s = sb1("g1_s", [P, KC])
        g2_s = sb1("g2_s", [P, KC])
        one_s = sb1("one_s", [P, KC])
        bias_f = sb1("bias_f", [3, NBIAS])
        bias_l = sb1("bias_l", [3, NBIAS])
        bias_p = sb1("bias_p", [3, NBIAS], BF16)
        bias_a = sb1("bias_a", [3, NBIAS])
        pick = sb1("pick", [3, 3])
        am_f = sb1("am_f", [4, P + 512])
        fm_f = sb1("fm_f", [2, P + 512])
        xbuf = [sb1(f"xbuf{b}", [P, FX]) for b in range(XB)]
        x_t = [halves1(f"x_t{b}", [P, XC, P]) for b in range(2)]
        plain_mv = sb1("plain_mv", [P, 2])
        mixed_mv = sb1("mixed_mv", [P, 2])

        bank = [ctx.enter_context(nc.psum_tensor(f"bank{n}", [P, 512], F32)) for n in range(8)]

        def product(dst, a_h, a_l, b_h, b_l, chunks, start=True, stop=True):
            for c in range(chunks):
                nc.tensor.matmul(dst, a_h(c), b_h(c), start=start and c == 0, stop=False)
                nc.tensor.matmul(dst, a_h(c), b_l(c), start=False, stop=False)
                last = nc.tensor.matmul(dst, a_l(c), b_h(c), start=False, stop=stop and c == chunks - 1)
            return last

        def rows_times(dst, t_h, t_l, w_h, w_l, bias=None):
            last = product(dst, lambda c: t_h[:, c, :], lambda c: t_l[:, c, :], w_h, w_l, KC, stop=bias is None)
            if bias is not None:
                last = nc.tensor.matmul(dst, ones3[:, :], brow[:, bias], start=False, stop=True)
            return last

        w_in, b_in, tokw_in, c_in, txt_in, txt_zero = (sem(n) for n in ("w_in", "b_in", "tokw_in", "c_in", "txt_in", "txt_zero"))
        x_in = [sem(f"x_in{b}") for b in range(XB)]
        tokw_f, tokw_hi, tokw_ready = sem("tokw_f"), sem("tokw_hi"), sem("tokw_ready")
        consts_ready, link1, w_steps = sem("consts_ready"), sem("link1"), sem("w_steps")
        front_done, back_done = sem("front_done"), sem("back_done")
        hi_ready, lo_ready = sem("hi_ready"), sem("lo_ready")
        mix_done, h_ready, st_ready, mv_ready, cf_ready = (sem(n) for n in ("mix_done", "h_ready", "st_ready", "mv_ready", "cf_ready"))
        veps_ready, rs_ready, st_txt, mv_txt = sem("veps_ready"), sem("rs_ready"), sem("st_txt"), sem("mv_txt")
        txt_tiles = TILES - IMG_TILES
        early = IMG_TILES - 4

        with nc.Block() as block:
            @block.sync
            def _(sp):
                sp.dma_start(ident[:, :], ident_c).then_inc(c_in, 16)
                for b in range(XB):
                    sp.dma_start(xbuf[b][:, :], x[b * P:(b + 1) * P, :]).then_inc(x_in[b], 16)
                with sp.Fori(1, IMG_TILES // XB) as g:
                    for b in range(XB):
                        sp.wait_ge(back_done, (g - 1) * XB + b + 1)
                        sp.dma_start(xbuf[b][:, :], x[bass.ds(g * (XB * P) + b * P, P), :]).then_inc(x_in[b], 16)

            @block.scalar
            def _(act):
                act.dma_start(tokd[:, :], w_t.unsqueeze(0).to_broadcast([32, 4, D])).then_inc(tokw_in, 16)
                for c in range(XC):
                    src = ws_t[c * 32:(c + 1) * 32, :].unsqueeze(1).to_broadcast([32, 4, D])
                    act.dma_start(tokw[:, c, :], src).then_inc(tokw_in, 16)
                full = TILES - 1 - IMG_TILES
                act.wait_ge(txt_zero, 1)
                act.dma_start(h_all[:, IMG_TILES:TILES - 1, :],
                              txt[0:full * P, :].rearrange("(n p) f -> p n f", p=P)).then_inc(txt_in, 16)
                act.dma_start(h_all[0:TAIL, TILES - 1, :], txt[full * P:full * P + TAIL, :]).then_inc(txt_in, 16)
                for dst, src in (
                    (bias_f[:, 0:3 * D], in_b.unsqueeze(0).to_broadcast([3, 3 * D])),
                    (bias_f[:, 3 * D:4 * D], out_b.unsqueeze(0).to_broadcast([3, D])),
                    (bias_f[:, 4 * D:5 * D], bq.unsqueeze(0).to_broadcast([3, D])),
                    (bias_f[:, 5 * D:6 * D], bo.unsqueeze(0).to_broadcast([3, D])),
                    (bias_f[:, 6 * D:6 * D + E], bg.unsqueeze(0).to_broadcast([3, E])),
                    (pick[:, :], pick_c),
                    (ls[:, :], logit.unsqueeze(0).to_broadcast([P, H])),
                ):
                    act.dma_start(dst, src).then_inc(b_in, 16)
                act.wait_ge(tokw_f, 1)
                nc.scalar.activation(tokw_h[:, :, :], tokw[:, :, :], ACT.Copy).then_inc(tokw_hi, 1)
                weights = (
                    (inw[:, :, :], in_w.rearrange("(c p) n -> p c n", p=P)),
                    (outw[:, :, :], out_w.rearrange("(c p) n -> p c n", p=P)),
                    (headw[:, :], head),
                    (wq_s[:, :, :], wq.rearrange("(c p) n -> p c n", p=P)),
                    (wd_s[:, :, :], wd.rearrange("(c p) n -> p c n", p=P)),
                    (wu_s[0:LAT, :], wu),
                    (wu_s[LAT:LAT + 1, :], bu.unsqueeze(0)),
                    (wo_s[:, :, :], wo.rearrange("(c p) n -> p c n", p=P)),
                    (wg_s[:, :, :], wg.rearrange("(c p) n -> p c n", p=P)),
                    (we_s[:, 0, :, :], we[:, 0:P, :].rearrange("e p f -> p e f")),
                    (we_s[:, 1, :, :], we[:, P:D, :].rearrange("e p f -> p e f")),
                    (g1_s[:, :], g1), (g2_s[:, :], g2),
                    (bd_s[:, :], bd.unsqueeze(1)),
                    (am_f[:, :], amask_c), (fm_f[:, :], fmask_c),
                )
                assert len(weights) == 16
                for dst, src in weights:
                    act.dma_start(dst, src).then_inc(w_in, 16)

                def high(i, p):
                    wait(act, mix_done, i - 1)
                    act.wait_ge(front_done, i + 1)
                    nc.scalar.activation(x_t[p][0][:, 0:4, :], bank[2 * p][:, :], ACT.Copy).then_inc(hi_ready, 1)
                    act.wait_ge(back_done, i + 1)
                    nc.scalar.activation(x_t[p][0][:, 4:8, :], bank[2 * p + 1][:, :], ACT.Copy).then_inc(hi_ready, 1)

                for b in range(XB):
                    high(b, b % 2)
                with act.Fori(1, IMG_TILES // XB) as g:
                    for b in range(XB):
                        high(g * XB + b, b % 2)

            @block.gpsimd
            def _(pool):
                nc.gpsimd.memset(h_all[96:128, TILES - 1, :], 0.0).then_inc(txt_zero, 1)
                pool.wait_ge(txt_zero, 1)
                nc.gpsimd.memset(neghalf[:, :], -0.5)
                nc.gpsimd.memset(onehalf[:, :], 1.5)
                nc.gpsimd.memset(ln_eps[:, :], LN_EPS)
                nc.gpsimd.memset(rms_eps[:, :], RMS_EPS)
                nc.gpsimd.memset(one_s[:, :], 1.0)
                nc.gpsimd.memset(ones3[:, :], 1.0)
                nc.gpsimd.memset(plain_mv[:, :], 1.0)
                nc.gpsimd.memset(mixed_mv[:, 0:1], 1.0 / WS)
                nc.gpsimd.memset(mixed_mv[:, 1:2], 1.0 / WS ** 2)
                nc.gpsimd.memset(kpad[:, :, :, :], 0.0)
                nc.gpsimd.memset(qpad[:, :, :], 0.0)
                for p in range(2):
                    nc.gpsimd.memset(vaug[p][:, :, HD:HD + 1], 1.0)
                    nc.gpsimd.memset(v48[p][:, :, 33:48], 0.0)
                    last = nc.gpsimd.memset(v48[p][:, :, 32:33], 1.0)
                last.then_inc(consts_ready, 1)
                pool.wait_ge(consts_ready, 1)
                nc.gpsimd.memset(lat[LAT:LAT + 1, :], 1.0).then_inc(consts_ready, 1)
                pool.wait_ge(consts_ready, 2)
                pool.wait_ge(w_in, 16 * 16)
                todo = [(w, w_h, w_l, gain, scale, c)
                        for w, w_h, w_l, gain, scale in ((inw, inw_h, inw_l, one_s, WS), (outw, outw_h, outw_l, headw, WS),
                                                         (wq_s, wq_h, wq_l, g1_s, WS), (wd_s, wd_h, wd_l, g1_s, WS),
                                                         (wo_s, wo_h, wo_l, one_s, WS), (wg_s, wg_h, wg_l, g2_s, 1.0),
                                                         (we_s, we_h, we_l, g2_s, WS))
                        for c in range(KC)]
                for w, _, _, gain, scale, c in todo:
                    last = nc.gpsimd.tensor_scalar(w[:, c], w[:, c], gain[:, c:c + 1], scale, ALU.mult, ALU.mult)
                last.then_inc(w_steps, 1)
                pool.wait_ge(w_steps, 1)
                for w, w_h, _, _, _, c in todo:
                    last = nc.gpsimd.tensor_copy(w_h[:, c], w[:, c])
                last.then_inc(w_steps, 1)
                pool.wait_ge(w_steps, 2)
                for w, w_h, w_l, _, _, c in todo:
                    nc.gpsimd.tensor_tensor(w_l[:, c], w[:, c], w_h[:, c], ALU.subtract)
                nc.gpsimd.tensor_copy(am[:, :], am_f[:, :])
                nc.gpsimd.tensor_copy(fm[:, :], fm_f[:, :]).then_inc(consts_ready, 1)

                for n, (lo, hi, need) in enumerate(((0, early, txt_tiles + early), (early, TILES, TILES))):
                    pool.wait_ge(cf_ready, need)
                    var = cf_all[:, lo:hi, RS:RS + 1].squeeze(2)
                    nc.gpsimd.tensor_tensor(var, var, ln_eps[:, :].to_broadcast([P, hi - lo]), ALU.add).then_inc(veps_ready, 1)
                    pool.wait_ge(veps_ready, n + 1)
                    nc.gpsimd.tensor_tensor(var, var, neghalf[:, lo:hi], ALU.pow).then_inc(rs_ready, 1)
                pool.wait_ge(rs_ready, 2)

            @block.vector
            def _(dve):
                dve.wait_ge(tokw_in, 16 * (XC + 1))
                nc.vector.scalar_tensor_tensor(out=tokw[:, :, :], in0=tokw[:, :, :], scalar=WS,
                                               in1=tokd[:, :].unsqueeze(1).to_broadcast([P, XC, D]),
                                               op0=ALU.mult, op1=ALU.mult).then_inc(tokw_f, 1)
                dve.wait_ge(tokw_hi, 1)
                nc.vector.tensor_tensor(tokw_l[:, :, :], tokw[:, :, :], tokw_h[:, :, :], ALU.subtract).then_inc(tokw_ready, 1)

                def low(i, p):
                    for half in range(2):
                        dve.wait_ge(hi_ready, i * 2 + half + 1)
                        nc.vector.tensor_tensor(x_t[p][1][:, 4 * half:4 * half + 4, :], bank[2 * p + half][:, :],
                                                x_t[p][0][:, 4 * half:4 * half + 4, :], ALU.subtract).then_inc(lo_ready, 1)

                def stats(row, taken):
                    nc.vector.bn_stats(st[:, :], row).then_inc(taken, 1)

                def stats_kept(n, at, unscale, taken, together):
                    settle(dve, tokw_ready)
                    dve.wait_ge(taken, n)
                    nc.vector.bn_aggr(mv[:, :], st[:, :]).then_inc(together, 1)
                    dve.wait_ge(together, n)
                    nc.vector.tensor_tensor(at, mv[:, :], unscale[:, :], ALU.mult).then_inc(cf_ready, 1)

                def take(i, p):
                    dve.wait_ge(mix_done, i + 1)
                    stats(bank[4 + p][:, 0:D], st_ready)
                    nc.vector.tensor_scalar(h_all[:, bass.ds(i, 1), :].squeeze(1), bank[4 + p][:, 0:D], 1.0 / WS, None,
                                            ALU.mult).then_inc(h_ready, 1)
                    stats_kept(i + 1, cf_all[:, bass.ds(i, 1), 0:2].squeeze(1), mixed_mv, st_ready, mv_ready)

                dve.wait_ge(txt_in, 32)
                dve.wait_ge(consts_ready, 2)
                for n in range(txt_tiles):
                    stats(h_all[:, IMG_TILES + n, :], st_txt)
                    stats_kept(n + 1, cf_all[:, IMG_TILES + n, 0:2], plain_mv, st_txt, mv_txt)
                for b in range(XB):
                    low(b, b % 2)
                    if b:
                        take(b - 1, (b - 1) % 2)
                with dve.Fori(1, IMG_TILES // XB) as g:
                    for b in range(XB):
                        low(g * XB + b, b % 2)
                        take(g * XB + b - 1, (b - 1) % 2)
                dve.wait_ge(b_in, 16 * 7)
                n = 0

                def linked(op):
                    nonlocal n
                    n += 1
                    op.then_inc(link1, 1)
                    dve.wait_ge(link1, n)

                linked(nc.vector.tensor_scalar(bias_f[:, 0:6 * D], bias_f[:, 0:6 * D], WS, None, ALU.mult))
                left = bias_f
                for k in range(3):
                    linked(nc.vector.tensor_copy(bias_p[:, :], left[:, :]))
                    if k < 2:
                        linked(nc.vector.tensor_tensor(bias_l[:, :], left[:, :], bias_p[:, :], ALU.subtract))
                    if k == 0:
                        linked(nc.vector.tensor_scalar(bias_a[:, :], bias_p[:, :], pick[:, 0:1], None, ALU.mult))
                    else:
                        linked(nc.vector.scalar_tensor_tensor(out=bias_a[:, :], in0=bias_p[:, :], scalar=pick[:, k:k + 1],
                                                              in1=bias_a[:, :], op0=ALU.mult, op1=ALU.add))
                    left = bias_l
                nc.vector.tensor_copy(brow[:, :], bias_a[:, :])
                linked(nc.vector.tensor_scalar(ls[:, :], ls[:, :], 4.605170185988091, None, ALU.min))
                take(IMG_TILES - 1, (IMG_TILES - 1) % 2)

            @block.tensor
            def _(pe):
                def turn(i, p, b, full):
                    pe.wait_ge(x_in[b], full)
                    for c in range(XC):
                        half = nc.tensor.transpose(bank[2 * p + c // 4][:, (c % 4) * P:(c % 4 + 1) * P],
                                                   xbuf[b][:, c * P:(c + 1) * P], ident[:, :])
                        if c == 3:
                            half.then_inc(front_done, 1)
                    half.then_inc(back_done, 1)

                def mix(i, p):
                    pe.wait_ge(lo_ready, i * 2 + 2)
                    wait(pe, h_ready, i - 1)
                    t_h, t_l = x_t[p]
                    product(bank[4 + p][:, 0:D], lambda c: t_h[:, c, :], lambda c: t_l[:, c, :],
                            lambda c: tokw_h[:, c, :], lambda c: tokw_l[:, c, :], XC).then_inc(mix_done, 1)

                pe.wait_ge(c_in, 16)
                for b in range(XB):
                    turn(b, b % 2, b, 16)
                    if b == 1:
                        pe.wait_ge(tokw_ready, 1)
                    if b:
                        mix(b - 1, (b - 1) % 2)
                with pe.Fori(1, IMG_TILES // XB) as g:
                    for b in range(XB):
                        turn(g * XB + b, b % 2, b, g * 16 + 16)
                        mix(g * XB + b - 1, (b - 1) % 2)
                mix(IMG_TILES - 1, (IMG_TILES - 1) % 2)

        phase1.close()
        xn = sb("xn", [P, D])
        xt_h, xt_l = halves("xt", [P, KC, P])
        sq = sb("sq", [P, 2 * H, HD])
        ss = sb("ss", [P, 2 * H])
        half_ss = sb("half_ss", [P, 2 * H])
        shifted = sb("shifted", [P, 2 * H])
        rn = sb("rn", [P, 2 * H])
        rt = sb("rt", [P, 2 * H])
        qkr = [sb(f"qkr{p}", [P, 2 * D]) for p in range(2)]
        qn = sb("qn", [P, H, HD])
        q_t = sb("q_t", [P, 8, 32])
        k_t = sb("k_t", [P, 8, 64])
        smax = sb("smax", [P, 16])
        sc = sb("sc", [P, 16, 32])
        pr = sb("pr", [P, 16, 32])
        pr_t = sb("pr_t", [P, 16, 32])
        rsum = sb("rsum", [P, H])
        on = sb("on", [P, H, HD])
        on_h, on_l = halves("on_t", [P, KC, P])
        cf = sb("cf", [P, 4])
        vtmp = sb("vtmp", [P, 1])
        ms = sb("ms", [P, 1])
        mse = sb("mse", [P, 1])
        ms2 = sb("ms2", [P, 1])
        x1 = sb("x1", [P, D])
        hn = sb("hn", [P, D])
        hn_h, hn_l = halves("hn_t", [P, KC, P])
        fq_t = sb("fq_t", [P, 32, H])
        kv_t = sb("kv_t", [P, H, 32])
        of = sb("of", [P, H, 32])
        x2 = sb("x2", [P, D])
        hx2 = [sb(f"hx2_{p}", [P, D]) for p in range(2)]
        junk = sb("junk", [P, D])
        ss2 = sb("ss2", [P, 1])
        t2 = sb("t2", [P, 1])
        r2 = sb("r2", [P, 1])
        h2 = sb("h2", [P, D])
        h2_t = [halves(f"h2_t{p}", [P, KC, P]) for p in range(2)]
        gmax = sb("gmax", [P, 1])
        gexp = sb("gexp", [P, E])
        gsum = sb("gsum", [P, 1])
        grec = sb("grec", [P, 1])
        gate = [sb(f"gate{p}", [P, E]) for p in range(2)]
        acc = sb("acc", [P, D])
        res = sb("res", [P, D])

        names = ("ls_ready", "a_xn", "a_xnps", "a_xth", "a_xtl", "a_qkv", "a_sq", "a_qkr", "a_v", "a_ss", "a_half",
                 "a_shift", "a_guess", "a_lsq", "a_qk", "a_qkt", "a_s", "a_max", "a_sub", "a_exp", "a_prt", "a_av", "a_rsum",
                 "a_on", "a_onps", "a_onh", "a_onl", "a_out", "a_h", "a_st", "a_mv", "p_newton", "p_rn", "p_var", "p_rs",
                 "p_ms", "p_mse", "p_rms", "p_rr", "p_all")
        (ls_ready, a_xn, a_xnps, a_xth, a_xtl, a_qkv, a_sq, a_qkr, a_v, a_ss, a_half,
         a_shift, a_guess, a_lsq, a_qk, a_qkt, a_s, a_max, a_sub, a_exp, a_prt, a_av, a_rsum,
         a_on, a_onps, a_onh, a_onl, a_out, a_h, a_st, a_mv, p_newton, p_rn, p_var, p_rs,
         p_ms, p_mse, p_rms, p_rr, p_all) = map(sem, names)
        b_xt, b_qk, b_v, b_s, b_o, b_ot, b_out = bank[0:7]

        with nc.Block() as block:
            @block.tensor
            def _(pe):
                def body(i, p):
                    if real(i, 0):
                        pe.wait_ge(a_qkt, i + 1)
                        nc.tensor.matmul(b_s[:, :], am[:, 0:P], am[:, P:], start=True, stop=True,
                                         skip_group_check=True)
                        for pair in range(8):
                            for j in range(4):
                                q = slice(32 * j, 32 * j + 32)
                                last = nc.tensor.matmul(b_s[q, pair * 64:pair * 64 + 64], q_t[q, pair, :], k_t[q, pair, :],
                                                        start=False, stop=True, skip_group_check=True)
                        last.then_inc(a_s, 1)
                    if real(i, -1):
                        pe.wait_ge(a_on, i)
                        for c in range(KC):
                            last = nc.tensor.transpose(b_ot[:, c * P:(c + 1) * P],
                                                       on[:, :, :].rearrange("p h d -> p (h d)")[:, c * P:(c + 1) * P],
                                                       ident[:, :])
                        last.then_inc(a_onps, 1)
                    if real(i, 2):
                        pe.wait_ge(a_xtl, i + 3)
                        wait(pe, a_qkr, i + 2)
                        wait(pe, a_v, i + 2)
                        for dst, n0, n1 in ((b_qk, 0, 2 * D), (b_v, 2 * D, 3 * D)):
                            last = rows_times(dst[:, 0:n1 - n0], xt_h, xt_l, lambda c: inw_h[:, c, n0:n1],
                                              lambda c: inw_l[:, c, n0:n1], slice(n0, n1))
                        last.then_inc(a_qkv, 1)
                    if real(i, -1):
                        pe.wait_ge(a_onl, i)
                        wait(pe, a_h, i - 1)
                        rows_times(b_out[:, 0:D], on_h, on_l, lambda c: outw_h[:, c, :], lambda c: outw_l[:, c, :],
                                   slice(3 * D, 4 * D)).then_inc(a_out, 1)
                    if real(i, 0):
                        settle(pe, c_in)
                        pe.wait_ge(a_prt, i + 1)
                        pe.wait_ge(a_v, i + 1)
                        for h in range(H):
                            for j in range(4):
                                q = slice(32 * j, 32 * j + 32)
                                last = nc.tensor.matmul(b_o[q, h * 17:h * 17 + 17], pr_t[q, h, :], vaug[p][q, h, :],
                                                        start=True, stop=True)
                        last.then_inc(a_av, 1)
                    if real(i, 3):
                        pe.wait_ge(a_xn, i + 4)
                        for c in range(KC):
                            last = nc.tensor.transpose(b_xt[:, c * P:(c + 1) * P], xn[:, c * P:(c + 1) * P], ident[:, :])
                        last.then_inc(a_xnps, 1)

                tiles_in_order(pe, body, 1, 3)

            @block.scalar
            def _(act):
                nc.scalar.activation(ls[:, :], ls[:, :], ACT.Exp).then_inc(ls_ready, 1)

                def body(i, p):
                    if real(i, -1):
                        act.wait_ge(a_onps, i)
                        wait(act, a_out, i - 1)
                        nc.scalar.activation(on_h[:, :, :], b_ot[:, 0:D], ACT.Copy).then_inc(a_onh, 1)
                    if real(i, 0):
                        act.wait_ge(a_sub, i + 1)
                        wait(act, a_prt, i)
                        nc.scalar.activation(pr[:, :, :], sc[:, :, :], ACT.Exp).then_inc(a_exp, 1)
                    if real(i, 2):
                        act.wait_ge(a_qkv, i + 3)
                        wait(act, a_ss, i + 2)
                        nc.scalar.activation(sq[:, :, :], b_qk[:, :], ACT.Square, scale=1.0 / WS).then_inc(a_sq, 1)
                        wait(act, a_qk, i + 1)
                        nc.scalar.activation(qkr[p][:, :], b_qk[:, :], ACT.Copy, scale=1.0 / WS).then_inc(a_qkr, 1)
                        wait(act, a_av, i + 1)
                        nc.scalar.activation(vaug[p][:, :, 0:HD], b_v[:, 0:D], ACT.Copy, scale=1.0 / WS).then_inc(a_v, 1)
                    if real(i, 3):
                        act.wait_ge(a_xnps, i + 4)
                        wait(act, a_qkv, i + 3)
                        nc.scalar.activation(xt_h[:, :, :], b_xt[:, 0:D], ACT.Copy).then_inc(a_xth, 1)

                tiles_in_order(act, body, 1, 3)

            @block.vector
            def _(dve):
                def body(i, p):
                    if real(i, 2):
                        dve.wait_ge(a_xth, i + 3)
                        nc.vector.tensor_tensor(xt_l[:, :, :], b_xt[:, 0:D], xt_h[:, :, :], ALU.subtract).then_inc(a_xtl, 1)
                    if real(i, 1):
                        dve.wait_ge(a_sq, i + 2)
                        wait(dve, p_rn, i + 1)
                        nc.vector.tensor_reduce(ss[:, :], sq[:, :, :], AX.X, ALU.add).then_inc(a_ss, 1)
                    if real(i, 3):
                        wait(dve, a_xnps, i + 3)
                        at = bass.ds(i + 3, 1)
                        nc.vector.tensor_scalar(xn[:, :], h_all[:, at, :].squeeze(1), cf_all[:, at, MEAN:MEAN + 1].squeeze(1),
                                                cf_all[:, at, RS:RS + 1].squeeze(1), ALU.subtract, ALU.mult).then_inc(a_xn, 1)
                    if real(i, 1):
                        dve.wait_ge(a_ss, i + 2)
                        nc.vector.tensor_scalar(half_ss[:, :], ss[:, :], 1e-24, 0.5, ALU.max, ALU.mult).then_inc(a_half, 1)
                        dve.wait_ge(a_half, i + 2)
                        nc.vector.tensor_scalar(shifted[:, :].bitcast(U32), half_ss[:, :].bitcast(U32), 1, None,
                                                ALU.logical_shift_right).then_inc(a_shift, 1)
                    if real(i, -1):
                        dve.wait_ge(a_onh, i)
                        wait(dve, a_out, i - 1)
                        nc.vector.tensor_tensor(on_l[:, :, :], b_ot[:, 0:D], on_h[:, :, :], ALU.subtract).then_inc(a_onl, 1)
                    if real(i, 1):
                        dve.wait_ge(a_shift, i + 2)
                        nc.vector.tensor_scalar(rn[:, :].bitcast(I32), shifted[:, :].bitcast(I32), -1.0,
                                                float(RSQRT_MAGIC - (1 << 22)), ALU.mult, ALU.add).then_inc(a_guess, 1)
                    if real(i, 0):
                        dve.wait_ge(a_s, i + 1)
                        s3 = b_s[:, :].rearrange("p (h m) -> p h m", h=H)
                        nc.vector.tensor_reduce(smax[:, :], s3, AX.X, ALU.max).then_inc(a_max, 1)
                        dve.wait_ge(a_max, i + 1)
                        wait(dve, a_exp, i)
                        nc.vector.tensor_tensor(sc[:, :, :], s3, smax[:, :].unsqueeze(2).to_broadcast([P, H, 32]),
                                                ALU.subtract).then_inc(a_sub, 1)
                    if real(i, 1):
                        dve.wait_ge(p_rn, i + 2)
                        if isinstance(i, int) and i == -1:
                            dve.wait_ge(ls_ready, 1)
                        nc.vector.tensor_tensor(rn[:, 0:H], rn[:, 0:H], ls[:, :], ALU.mult).then_inc(a_lsq, 1)
                        dve.wait_ge(a_qkr, i + 2)
                        raw = qkr[1 - p]
                        nc.vector.tensor_tensor(kpad[:, :, 0:4:3, :], raw[:, D:2 * D].rearrange("p (a s d) -> p a s d", s=2, d=HD),
                                                rn[:, H:].rearrange("p (a s) -> p a s", s=2).unsqueeze(3).to_broadcast([P, 8, 2, HD]),
                                                ALU.mult)
                        dve.wait_ge(a_lsq, i + 2)
                        nc.vector.tensor_tensor(qn[:, :, :], raw[:, 0:D].rearrange("p (h d) -> p h d", d=HD),
                                                rn[:, 0:H].unsqueeze(2).to_broadcast([P, H, HD]),
                                                ALU.mult).then_inc(a_qk, 1)
                    if real(i, 0):
                        dve.wait_ge(a_exp, i + 1)
                        wait(dve, a_av, i)
                        nc.vector.transpose(pr_t[:, :, :], pr[:, :, :]).then_inc(a_prt, 1)
                    if real(i, 1):
                        dve.wait_ge(a_qk, i + 2)
                        nc.vector.transpose(k_t[:, :, :], kpad[:, :, :, :])
                        nc.vector.transpose(q_t[:, :, :], qn[:, :, :]).then_inc(a_qkt, 1)
                    if real(i, -1):
                        dve.wait_ge(a_out, i)
                        hi = h_all[:, bass.ds(i - 1, 1), :].squeeze(1)
                        nc.vector.scalar_tensor_tensor(out=hi, in0=b_out[:, 0:D], scalar=1.0 / WS, in1=hi,
                                                       op0=ALU.mult, op1=ALU.add).then_inc(a_h, 1)
                        settle(dve, tokw_ready)
                        dve.wait_ge(a_h, i)
                        nc.vector.bn_stats(st[:, :], hi).then_inc(a_st, 1)
                        settle(dve, tokw_ready)
                        dve.wait_ge(a_st, i)
                        wait(dve, p_ms, i - 1)
                        nc.vector.bn_aggr(mv[:, :], st[:, :]).then_inc(a_mv, 1)
                    if real(i, 0):
                        dve.wait_ge(a_av, i + 1)
                        o3 = b_o[:, 0:H * 17].rearrange("p (h d) -> p h d", d=17)
                        nc.vector.reciprocal(rsum[:, :], o3[:, :, HD:HD + 1]).then_inc(a_rsum, 1)
                        dve.wait_ge(a_rsum, i + 1)
                        wait(dve, a_onps, i)
                        nc.vector.tensor_tensor(on[:, :, :], o3[:, :, 0:HD], rsum[:, :].unsqueeze(2).to_broadcast([P, H, HD]),
                                                ALU.mult).then_inc(a_on, 1)

                tiles_in_order(dve, body, 1, 3)

            @block.gpsimd
            def _(pool):
                def body(i, p):
                    if real(i, 1):
                        n = 11 * (i + 1)
                        for k in range(3):
                            for m, (o, a, b, op) in enumerate(((rt, rn, rn, ALU.mult), (rt, rt, half_ss, ALU.mult),
                                                               (rt, onehalf, rt, ALU.subtract), (rn, rn, rt, ALU.mult))):
                                if k == 0 and m == 0:
                                    pool.wait_ge(a_guess, i + 2)
                                else:
                                    pool.wait_ge(p_newton, n + 4 * k + m)
                                step = nc.gpsimd.tensor_tensor(o[:, :], a[:, :], b[:, :], op)
                                step.then_inc(p_newton if (k, m) != (2, 3) else p_rn, 1)
                    if real(i, -1):
                        pool.wait_ge(a_mv, i)
                        nc.gpsimd.tensor_tensor(vtmp[:, :], mv[:, 1:2], ln_eps[:, :], ALU.add).then_inc(p_var, 1)
                        wait(pool, p_all, i - 1)
                        pool.wait_ge(p_var, i)
                        nc.gpsimd.tensor_tensor(cf[:, RS:RS + 1], vtmp[:, :], neghalf[:, 0:1], ALU.pow).then_inc(p_rs, 1)
                        settle(pool, consts_ready)
                        pool.wait_ge(p_rs, i)
                        nc.gpsimd.tensor_scalar(ms[:, :], mv[:, 1:2], cf[:, RS:RS + 1], cf[:, RS:RS + 1], ALU.mult, ALU.mult)
                        nc.gpsimd.tensor_copy(cf[:, MEAN:MEAN + 1], mv[:, 0:1])
                        nc.gpsimd.tensor_scalar(cf[:, NM:NM + 1], mv[:, 0:1], cf[:, RS:RS + 1], -1.0, ALU.mult,
                                                ALU.mult).then_inc(p_ms, 1)
                        pool.wait_ge(p_ms, i)
                        nc.gpsimd.tensor_tensor(mse[:, :], ms[:, :], rms_eps[:, :], ALU.add).then_inc(p_mse, 1)
                        pool.wait_ge(p_mse, i)
                        nc.gpsimd.tensor_tensor(ms2[:, :], mse[:, :], neghalf[:, 0:1], ALU.pow).then_inc(p_rms, 1)
                        pool.wait_ge(p_rms, i)
                        nc.gpsimd.tensor_tensor(cf[:, RR:RR + 1], ms2[:, :], cf[:, RS:RS + 1], ALU.mult).then_inc(p_rr, 1)
                        settle(pool, consts_ready)
                        pool.wait_ge(p_rr, i)
                        nc.gpsimd.tensor_copy(cf_all[:, bass.ds(i - 1, 1), :], cf[:, :].unsqueeze(1)).then_inc(p_all, 1)

                tiles_in_order(pool, body, 1, 3)

        names = ("f_hn", "f_hnps", "f_hth", "f_htl", "f_q", "f_down", "f_lat", "f_qpad", "f_kv", "f_kvt", "f_qt",
                 "f_s", "f_max", "f_sub", "f_exp", "f_prt", "f_av", "f_of", "f_rsum", "f_on", "f_onps", "f_onh", "f_onl",
                 "f_wo", "f_x2", "f_ss2", "f_h2", "f_h2ps", "f_h2h", "f_h2l", "f_gate", "f_gmax", "f_gexp", "f_grec",
                 "f_gmul", "f_we", "f_comb", "f_acc", "f_x1", "p_hx2", "p_t2", "p_r2", "out_done")
        (f_hn, f_hnps, f_hth, f_htl, f_q, f_down, f_lat, f_qpad, f_kv, f_kvt, f_qt,
         f_s, f_max, f_sub, f_exp, f_prt, f_av, f_of, f_rsum, f_on, f_onps, f_onh, f_onl,
         f_wo, f_x2, f_ss2, f_h2, f_h2ps, f_h2h, f_h2l, f_gate, f_gmax, f_gexp, f_grec,
         f_gmul, f_we, f_comb, f_acc, f_x1, p_hx2, p_t2, p_r2, out_done) = map(sem, names)
        b_we, b_s, b_o, b_kv, b_turn, b_q, b_hn = bank[0:2], bank[2], bank[3], bank[4], bank[5], bank[6], bank[7]
        b_down, b_gate, b_wo = b_turn[0:LAT, D:D + P], b_q[:, D:D + E], b_hn[:, 0:D]
        EP = 2
        STEPS = E // EP

        with nc.Block() as block:
            @block.tensor
            def _(pe):
                def experts(i, p, steps):
                    if real(i, -2):
                        for s in steps:
                            wait(pe, f_comb, (i - 2) * STEPS + s - 1)
                            rows_times(b_we[s % 2][:, :], *h2_t[p], lambda c: we_h[:, c, s * EP:(s + 1) * EP, :],
                                       lambda c: we_l[:, c, s * EP:(s + 1) * EP, :]).then_inc(f_we, 1)

                def body(i, p):
                    if real(i, 0):
                        pe.wait_ge(f_qt, i + 1)
                        nc.tensor.matmul(b_s[:, :], fm[:, 0:P], fm[:, P:], start=True, stop=True,
                                         skip_group_check=True)
                        for pair in range(16):
                            for j in range(4):
                                q = slice(32 * j, 32 * j + 32)
                                last = nc.tensor.matmul(b_s[q, pair * 32:pair * 32 + 32],
                                                        fq_t[q, 2 * pair:2 * pair + 2, :].rearrange("r t h -> r (t h)"),
                                                        kv_t[q, :, 2 * pair:2 * pair + 2],
                                                        start=False, stop=True, skip_group_check=True)
                        last.then_inc(f_s, 1)
                    if real(i, 1):
                        pe.wait_ge(f_htl, i + 2)
                        wait(pe, f_gexp, i - 1)
                        rows_times(b_q[:, 0:D], hn_h, hn_l, lambda c: wq_h[:, c, :], lambda c: wq_l[:, c, :],
                                   slice(4 * D, 5 * D)).then_inc(f_q, 1)
                        wait(pe, f_onl, i)
                        product(b_down, lambda c: wd_h[:, c, :], lambda c: wd_l[:, c, :], lambda c: hn_h[:, c, :],
                                lambda c: hn_l[:, c, :], KC).then_inc(f_down, 1)
                    experts(i, p, range(0, STEPS // 2))
                    if real(i, -1):
                        pe.wait_ge(f_onl, i)
                        rows_times(b_wo, on_h, on_l, lambda c: wo_h[:, c, :], lambda c: wo_l[:, c, :],
                                   slice(5 * D, 6 * D)).then_inc(f_wo, 1)
                    if real(i, 1):
                        pe.wait_ge(f_lat, i + 2)
                        wait(pe, f_kvt, i + 1)
                        nc.tensor.matmul(b_kv[:, :], lat[:, :], wu_s[:, :], start=True, stop=True).then_inc(f_kv, 1)
                    if real(i, 0):
                        settle(pe, c_in)
                        pe.wait_ge(f_prt, i + 1)
                        wait(pe, f_of, i)
                        for pair in range(16):
                            for j in range(4):
                                q = slice(32 * j, 32 * j + 32)
                                last = nc.tensor.matmul(b_o[q, pair * 32:pair * 32 + 32], v48[p][q, pair, 16:48],
                                                        pr_t[q, pair, :], start=True, stop=True)
                        last.then_inc(f_av, 1)
                    if real(i, -1):
                        pe.wait_ge(f_h2, i)
                        for c in range(KC):
                            last = nc.tensor.transpose(b_turn[:, c * P:(c + 1) * P], h2[:, c * P:(c + 1) * P], ident[:, :])
                        last.then_inc(f_h2ps, 1)
                    if real(i, 2):
                        pe.wait_ge(f_hn, i + 3)
                        wait(pe, f_x2, i)
                        for c in range(KC):
                            last = nc.tensor.transpose(b_hn[:, c * P:(c + 1) * P], hn[:, c * P:(c + 1) * P], ident[:, :])
                        last.then_inc(f_hnps, 1)
                    experts(i, p, range(STEPS // 2, STEPS))
                    if real(i, -1):
                        pe.wait_ge(f_h2l, i)
                        if real(i, 1):
                            pe.wait_ge(f_qpad, i + 2)
                        rows_times(b_gate, *h2_t[1 - p], lambda c: wg_h[:, c, :], lambda c: wg_l[:, c, :],
                                   slice(6 * D, 6 * D + E)).then_inc(f_gate, 1)
                    if real(i, 0):
                        pe.wait_ge(f_on, i + 1)
                        wait(pe, f_h2l, i)
                        if real(i, 1):
                            pe.wait_ge(f_lat, i + 2)
                        for c in range(KC):
                            last = nc.tensor.transpose(b_turn[:, c * P:(c + 1) * P],
                                                       on[:, :, :].rearrange("p h d -> p (h d)")[:, c * P:(c + 1) * P],
                                                       ident[:, :])
                        last.then_inc(f_onps, 1)

                tiles_in_order(pe, body, 2, 3)

            @block.scalar
            def _(act):
                def body(i, p):
                    if real(i, -1):
                        act.wait_ge(f_onps, i)
                        wait(act, f_wo, i - 1)
                        nc.scalar.activation(on_h[:, :, :], b_turn[:, 0:D], ACT.Copy).then_inc(f_onh, 1)
                    if real(i, 1):
                        act.wait_ge(f_q, i + 2)
                        wait(act, f_qt, i + 1)
                        nc.scalar.activation(qpad[:, :, 0:HD], b_q[:, 0:D].rearrange("p (h d) -> p h d", d=HD), ACT.Copy,
                                             scale=1.0 / WS).then_inc(f_qpad, 1)
                    if real(i, 0):
                        act.wait_ge(f_sub, i + 1)
                        wait(act, f_prt, i)
                        nc.scalar.activation(pr[:, :, :], sc[:, :, :], ACT.Exp, scale=HD ** -0.5).then_inc(f_exp, 1)
                    if real(i, 1):
                        act.wait_ge(f_down, i + 2)
                        wait(act, f_kv, i + 1)
                        nc.scalar.activation(lat[0:LAT, :], b_down, ACT.Identity, bias=bd_s[:, :],
                                             scale=1.0 / WS).then_inc(f_lat, 1)
                    if real(i, -1):
                        act.wait_ge(f_x2, i)
                        wait(act, p_t2, i - 1)
                        nc.scalar.activation(junk[:, :], x2[:, :], ACT.Square, scale=D ** -0.5,
                                             accum_out=ss2[:, :]).then_inc(f_ss2, 1)
                    if real(i, 0):
                        settle(act, ls_ready)
                        wait(act, f_x2, i)
                        at = bass.ds(i, 1)
                        nc.scalar.activation(x1[:, :], h_all[:, at, :].squeeze(1), ACT.Identity,
                                             bias=cf_all[:, at, NM:NM + 1].squeeze(1),
                                             scale=cf_all[:, at, RS:RS + 1].squeeze(1)).then_inc(f_x1, 1)
                    if real(i, -1):
                        act.wait_ge(f_h2ps, i)
                        wait(act, f_gate, i - 2)
                        wait(act, f_we, (i - 2) * STEPS)
                        nc.scalar.activation(h2_t[1 - p][0][:, :, :], b_turn[:, 0:D], ACT.Copy).then_inc(f_h2h, 1)
                    if real(i, 2):
                        act.wait_ge(f_hnps, i + 3)
                        wait(act, f_down, i + 2)
                        nc.scalar.activation(hn_h[:, :, :], b_hn[:, 0:D], ACT.Copy).then_inc(f_hth, 1)
                    if real(i, -1):
                        act.wait_ge(f_gmax, i)
                        wait(act, f_gmul, i - 1)
                        nc.scalar.activation(gexp[:, :], b_gate, ACT.Exp, bias=gmax[:, :],
                                             accum_out=gsum[:, :]).then_inc(f_gexp, 1)

                tiles_in_order(act, body, 2, 3)

            @block.vector
            def _(dve):
                def combine(i, p, s):
                    if not real(i, -2):
                        return
                    dve.wait_ge(f_we, (i - 2) * STEPS + s + 1)
                    if s == 0:
                        dve.wait_ge(f_gmul, i - 1)
                        dve.wait_ge(p_hx2, i - 1)
                    else:
                        dve.wait_ge(f_comb, (i - 2) * STEPS + s)
                    for k in range(EP):
                        e = s * EP + k
                        if k:
                            dve.wait_ge(f_acc, (i - 2) * STEPS + s + 1)
                        if e == E - 1:
                            wait(dve, out_done, (i - 2) * 16)
                        op = nc.vector.scalar_tensor_tensor(
                            out=(res if e == E - 1 else acc)[:, :], in0=b_we[s % 2][:, k * D:(k + 1) * D],
                            scalar=gate[p][:, e:e + 1], in1=(acc if e else hx2[p])[:, :], op0=ALU.mult, op1=ALU.add)
                        op.then_inc(f_comb if k else f_acc, 1)

                def body(i, p):
                    if real(i, -1):
                        dve.wait_ge(f_onh, i)
                        nc.vector.tensor_tensor(on_l[:, :, :], b_turn[:, 0:D], on_h[:, :, :], ALU.subtract).then_inc(f_onl, 1)
                    if real(i, 0):
                        dve.wait_ge(f_s, i + 1)
                        s3 = b_s[:, :].rearrange("p (h m) -> p h m", m=32)
                        nc.vector.tensor_reduce(smax[:, :], s3, AX.X, ALU.max).then_inc(f_max, 1)
                        dve.wait_ge(f_max, i + 1)
                        wait(dve, f_exp, i)
                        nc.vector.tensor_tensor(sc[:, :, :], s3, smax[:, :].unsqueeze(2).to_broadcast([P, 16, 32]),
                                                ALU.subtract).then_inc(f_sub, 1)
                    combine(i, p, 0)
                    if real(i, 0):
                        dve.wait_ge(f_exp, i + 1)
                        wait(dve, f_av, i)
                        nc.vector.transpose(pr_t[:, :, :], pr[:, :, :]).then_inc(f_prt, 1)
                    combine(i, p, 1)
                    if real(i, -1):
                        dve.wait_ge(f_wo, i)
                        dve.wait_ge(f_x1, i)
                        wait(dve, p_hx2, i - 1)
                        wait(dve, f_ss2, i - 1)
                        nc.vector.scalar_tensor_tensor(out=x2[:, :], in0=b_wo, scalar=1.0 / WS, in1=x1[:, :],
                                                       op0=ALU.mult, op1=ALU.add).then_inc(f_x2, 1)
                    if real(i, 1):
                        dve.wait_ge(f_qpad, i + 2)
                        nc.vector.transpose(fq_t[:, :, :].rearrange("r t h -> r h t"), qpad[:, :, :])
                        dve.wait_ge(f_kv, i + 2)
                        nc.vector.transpose(kv_t[:, :, :], b_kv[:, :]).then_inc(f_kvt, 1)
                        dve.wait_ge(f_kvt, i + 2)
                    if real(i, -1):
                        dve.wait_ge(p_r2, i)
                        wait(dve, f_h2ps, i - 1)
                        nc.vector.tensor_scalar(h2[:, :], x2[:, :], r2[:, :], None, ALU.mult).then_inc(f_h2, 1)
                    if real(i, 1):
                        nc.vector.transpose(v48[1 - p][:, :, 0:32],
                                            kv_t[:, :, :].rearrange("r g (p t) -> r p g t", t=2)).then_inc(f_qt, 1)
                    if real(i, 0):
                        dve.wait_ge(f_av, i + 1)
                        nc.vector.transpose(of[:, :, :], b_o[:, :].rearrange("r (t h) -> r h t", h=H)).then_inc(f_of, 1)
                        dve.wait_ge(f_of, i + 1)
                        nc.vector.reciprocal(rsum[:, :], of[:, :, HD:HD + 1]).then_inc(f_rsum, 1)
                    if real(i, -1):
                        dve.wait_ge(f_h2h, i)
                        nc.vector.tensor_tensor(h2_t[1 - p][1][:, :, :], b_turn[:, 0:D], h2_t[1 - p][0][:, :, :],
                                                ALU.subtract).then_inc(f_h2l, 1)
                    if real(i, 0):
                        dve.wait_ge(f_rsum, i + 1)
                        wait(dve, f_onps, i)
                        nc.vector.tensor_tensor(on[:, :, :], of[:, :, 0:HD], rsum[:, :].unsqueeze(2).to_broadcast([P, H, HD]),
                                                ALU.mult).then_inc(f_on, 1)
                    combine(i, p, 2)
                    if real(i, 2):
                        dve.wait_ge(f_hth, i + 3)
                        nc.vector.tensor_tensor(hn_l[:, :, :], b_hn[:, 0:D], hn_h[:, :, :], ALU.subtract).then_inc(f_htl, 1)
                    if real(i, 3):
                        wait(dve, f_hnps, i + 3)
                        at = bass.ds(i + 3, 1)
                        nc.vector.tensor_scalar(hn[:, :], h_all[:, at, :].squeeze(1), cf_all[:, at, MEAN:MEAN + 1].squeeze(1),
                                                cf_all[:, at, RR:RR + 1].squeeze(1), ALU.subtract, ALU.mult).then_inc(f_hn, 1)
                    combine(i, p, 3)
                    if real(i, -1):
                        dve.wait_ge(f_gate, i)
                        nc.vector.tensor_reduce(gmax[:, :], b_gate, AX.X, ALU.max, negate=True).then_inc(f_gmax, 1)
                        dve.wait_ge(f_gexp, i)
                        nc.vector.reciprocal(grec[:, :], gsum[:, :]).then_inc(f_grec, 1)
                        dve.wait_ge(f_grec, i)
                        nc.vector.tensor_scalar(gate[1 - p][:, :], gexp[:, :], grec[:, :], 1.0 / WS, ALU.mult,
                                                ALU.mult).then_inc(f_gmul, 1)

                tiles_in_order(dve, body, 2, 3)

            @block.gpsimd
            def _(pool):
                def body(i, p):
                    if not real(i, 0):
                        return
                    hi = h_all[:, bass.ds(i, 1), :].squeeze(1)
                    pool.wait_ge(f_ss2, i + 1)
                    nc.gpsimd.tensor_tensor(t2[:, :], ss2[:, :], rms_eps[:, :], ALU.add).then_inc(p_t2, 1)
                    pool.wait_ge(p_t2, i + 1)
                    wait(pool, f_h2, i)
                    nc.gpsimd.tensor_tensor(r2[:, :], t2[:, :], neghalf[:, 0:1], ALU.pow).then_inc(p_r2, 1)
                    settle(pool, consts_ready)
                    wait(pool, f_acc, (i - 2) * STEPS + 1)
                    nc.gpsimd.tensor_tensor(hx2[p][:, :], hi, x2[:, :], ALU.add).then_inc(p_hx2, 1)

                tiles_in_order(pool, body, 0, 0)

            @block.sync
            def _(sp):
                with sp.Fori(0, TILES - 1) as i:
                    sp.wait_ge(f_comb, (i + 1) * STEPS)
                    sp.dma_start(out[bass.ds(i * P, P), :], res[:, :]).then_inc(out_done, 16)
                sp.wait_ge(f_comb, TILES * STEPS)
                sp.dma_start(out[(TILES - 1) * P:TOKENS, :], res[0:TAIL, :]).then_inc(out_done, 16)
                sp.wait_ge(out_done, TILES * 16)


def kernel(**inputs):
    import numpy as np
    import concourse.bacc as bacc
    from concourse.bass_utils import run_bass_kernel_spmd

    a = {n: np.asarray(v) for n, v in inputs.items()}

    def rows(t):
        return np.ascontiguousarray(np.swapaxes(t, 0, 1)).reshape(t.shape[0] * t.shape[1], -1)

    def columns(v):
        return v.reshape(KC, P).T

    p, c = np.arange(P), np.arange(512)

    def mask(group, of_row, of_column):
        k = np.arange(group)[:, None]
        return np.concatenate([(of_row(p) == k), (of_column(c) != k) * -BIG], axis=1).astype(np.float32)

    arrays = {
        "x": rows(a["x"].reshape(B, N_IMG, FX)), "txt": rows(a["txt"]),
        "ws_t": a["L0_tok_weighted_sum"].T, "w_t": a["L0_tok_weight"].T,
        "in_w": a["L0_attn_in_proj_weight"].T, "in_b": a["L0_attn_in_proj_bias"],
        "logit": a["L0_attn_logit_scale"].reshape(H),
        "head": columns(np.repeat(a["L0_attn_head_scale"].reshape(H), HD)),
        "out_w": a["L0_attn_out_w"].T, "out_b": a["L0_attn_out_b"],
        "g1": columns(a["L0_ffn_gamma1"]), "wq": a["L0_ffn_Wq"], "bq": a["L0_ffn_bq"],
        "wd": a["L0_ffn_Wdown"], "bd": a["L0_ffn_bdown"], "wu": a["L0_ffn_Wup"], "bu": a["L0_ffn_bup"],
        "wo": a["L0_ffn_Wo"], "bo": a["L0_ffn_bo"], "g2": columns(a["L0_ffn_gamma2"]),
        "wg": a["L0_ffn_Wg"], "bg": a["L0_ffn_bg"], "we": a["L0_ffn_We"],
        "ident_c": np.eye(P, dtype=np.float32),
        "amask_c": mask(4, lambda n: n % 32 // B, lambda n: n % 32 // B), "fmask_c": mask(2, lambda n: n % 32 // 16, lambda n: n % 2),
        "pick_c": np.eye(3, dtype=np.float32),
    }
    nc = bacc.Bacc("TRN2", target_bir_lowering=False, num_devices=1)
    put, args = {}, {}
    for name, v in arrays.items():
        put[f"in_{name}"] = np.ascontiguousarray(v)
        args[name] = nc.dram_tensor(f"in_{name}", v.shape, mybir.dt.from_np(v.dtype), kind="ExternalInput").ap()
    out = nc.dram_tensor("out", (TOKENS, D), F32, kind="ExternalOutput").ap()
    build(nc, out=out, **args)
    r = run_bass_kernel_spmd(nc, [put], core_ids=[0])
    got = r.results[0]["out"].reshape(N_IMG + N_TXT, B, D)
    return np.ascontiguousarray(np.swapaxes(got, 0, 1))
```

```python
import concourse.bass as bass
from concourse import mybir
from contextlib import ExitStack

F32 = mybir.dt.float32
BF16 = mybir.dt.bfloat16
F16 = mybir.dt.float16
U32 = mybir.dt.uint32
I32 = mybir.dt.int32
ALU = mybir.AluOpType
ACT = mybir.ActivationFunctionType
AX = mybir.AxisListType

P = 128
B = 8
N_IMG, N_TXT = 512, 77
D = 256
KC = D // P
H, HD = 16, 16
FX = D * 4
XC = FX // P
IMG_TILES = N_IMG * B // P
TOKENS = (N_IMG + N_TXT) * B
TILES = -(-TOKENS // P)
TAIL = TOKENS - (TILES - 1) * P
LAT = 64
E = 8
BIG = float(2 ** 120)
RSQRT_MAGIC = 0x5F3759DF
LN_EPS, RMS_EPS = 1e-5, 1e-6
MEAN, RS, NM, RR = range(4)
XB = 4
HEAD = range(TILES - 2, TILES + 1)
AHEAD = 4
WS = 256.0
NBIAS = 3 * D + D + D + D + E
BC = -(-NBIAS // P)




def wait(eng, sem, value):
    if not isinstance(value, int) or value > 0:
        eng.wait_ge(sem, value)


def settle(eng, sem):
    eng.wait_ge(sem, 1)


def tiles_in_order(eng, body, back, ahead, unroll=2, last_ahead=None, start=None, then=None):
    first = -(-(back + 1) // unroll) * unroll
    turns = (TILES - (last_ahead or ahead) - first) // unroll
    for i in range(-ahead if start is None else start, first):
        body(i, i % unroll)
    with eng.Fori(first // unroll, first // unroll + turns) as g:
        for p in range(unroll):
            body(g * unroll + p, p)
    for i in range(first + unroll * turns, TILES + back):
        body(i, i % unroll)
        if then:
            then(i)


def in_tail(head, i):
    if i in HEAD:
        turn = i - HEAD[-1] - 1
        head(turn, turn % 2)


def real(i, k):
    return not isinstance(i, int) or 0 <= i + k < TILES


def build(nc, x, txt, ws_rep, w_rep, in_w, logit, head, out_w, g1, wq, wd, bd, wu, bu, bv, bo, bq,
          wo, g2, wg, we, biases, bscale_c, ident_c, amask_c, fmask_c, out):
    with ExitStack() as ctx, ExitStack() as phase1:
        def sb(name, shape, dt=F32, stack=ctx):
            return stack.enter_context(nc.sbuf_tensor(name, shape, dt))

        def halves(name, shape):
            return sb(name + "_h", shape, F16), sb(name + "_l", shape, F16)

        def sem(name):
            return ctx.enter_context(nc.semaphore(name))

        h_all = sb("h_all", [P, TILES, D])
        cf_all = sb("cf_all", [P, TILES, 4])
        ident = sb("ident", [P, P])
        inw_h, inw_l = halves("inw", [P, KC, 3 * D])
        outw_h, outw_l = halves("outw", [P, KC, D])
        wq_h, wq_l = halves("wq", [P, KC, D])
        wd_h, wd_l = halves("wd", [P, KC, LAT])
        wu_h, wu_l = halves("wu", [LAT + 1, 2 * D])
        wo_h, wo_l = halves("wo", [P, KC, D])
        wg_h, wg_l = halves("wg", [P, KC, E])
        we_h, we_l = halves("we", [P, KC, E, D])
        ls = sb("ls", [P, H])
        bd_s = sb("bd_s", [LAT, 1])
        bv_h, bv_l = halves("bv", [P, KC, P])
        bvec = sb("bvec", [P, D])
        bo_s = sb("bo_s", [P, D])
        bq_s = sb("bq_s", [P, D])
        brow = sb("brow", [3, P * BC], BF16)
        ones3 = sb("ones3", [3, P], BF16)
        am = sb("am", [4, P + 512], BF16)
        fm = sb("fm", [2, P + 512], BF16)
        neghalf = sb("neghalf", [P, TILES])
        onehalf = sb("onehalf", [P, 2 * H])
        ln_eps = sb("ln_eps", [P, 1])
        rms_eps = sb("rms_eps", [P, 1])
        st = sb("st", [P, 6])
        mv = sb("mv", [P, 2])
        kpad = sb("kpad", [P, H // 2, 4, HD])
        vaug = [sb(f"vaug{p}", [P, H, HD + 1]) for p in range(3)]
        lat = sb("lat", [LAT + 1, P])
        lat_h, lat_l = halves("lat", [LAT + 1, P])
        qraw = sb("qraw", [P, D])
        qpad = sb("qpad", [P, H, 32])
        v48 = [sb(f"v48_{p}", [P, 16, 48]) for p in range(2)]

        def sb1(name, shape, dt=F32):
            return sb(name, shape, dt, phase1)

        def halves1(name, shape):
            return sb1(name + "_h", shape, F16), sb1(name + "_l", shape, F16)

        tokw = sb1("tokw", [P, XC, D])
        tokw_h, tokw_l = halves1("tokw", [P, XC, D])
        tokd = sb1("tokd", [P, D])
        inw = sb1("inw", [P, KC, 3 * D])
        outw = sb1("outw", [P, KC, D])
        headw = sb1("headw", [P, KC])
        wq_s = sb1("wq_s", [P, KC, D])
        wd_s = sb1("wd_s", [P, KC, LAT])
        wu_s = sb1("wu_s", [LAT + 1, 2 * D])
        wo_s = sb1("wo_s", [P, KC, D])
        wg_s = sb1("wg_s", [P, KC, E])
        we_s = sb1("we_s", [P, KC, E, D])
        g1_s = sb1("g1_s", [P, KC])
        g2_s = sb1("g2_s", [P, KC])
        one_s = sb1("one_s", [P, KC])
        bias_f = sb1("bias_f", [P, BC])
        bias_s = sb1("bias_s", [P, BC])
        bias_l = [sb1(f"bias_l{k}", [P, BC]) for k in range(3)]
        bias_p = [sb1(f"bias_p{k}", [P, BC], BF16) for k in range(3)]
        am_f = sb1("am_f", [4, P + 512])
        fm_f = sb1("fm_f", [2, P + 512])
        xbuf = [sb1(f"xbuf{b}", [P, FX]) for b in range(XB)]
        x_t = [halves1(f"x_t{b}", [P, XC, P]) for b in range(2)]
        warm = sb1("warm", [P, 1])
        bv_s = sb1("bv_s", [P, KC])
        plain_mv = sb1("plain_mv", [P, 2])
        mixed_mv = sb1("mixed_mv", [P, 2])

        bank = [ctx.enter_context(nc.psum_tensor(f"bank{n}", [P, 512], F32)) for n in range(8)]

        def product(dst, a_h, a_l, b_h, b_l, chunks, start=True, stop=True):
            for c in range(chunks):
                nc.tensor.matmul(dst, a_h(c), b_h(c), start=start and c == 0, stop=False)
                nc.tensor.matmul(dst, a_h(c), b_l(c), start=False, stop=False)
                last = nc.tensor.matmul(dst, a_l(c), b_h(c), start=False, stop=stop and c == chunks - 1)
            return last

        def rows_times(dst, t_h, t_l, w_h, w_l, bias=None):
            last = product(dst, lambda c: t_h[:, c, :], lambda c: t_l[:, c, :], w_h, w_l, KC, stop=bias is None)
            if bias is not None:
                last = nc.tensor.matmul(dst, ones3[:, :], brow[:, bias], start=False, stop=True)
            return last

        w_in, b_in, tokw_in, c_in, txt_in, txt_zero = (sem(n) for n in ("w_in", "b_in", "tokw_in", "c_in", "txt_in", "txt_zero"))
        x_in = [sem(f"x_in{b}") for b in range(XB)]
        tokw_f, tokw_hi, tokw_ready = sem("tokw_f"), sem("tokw_hi"), sem("tokw_ready")
        ls_min, bv_ready = sem("ls_min"), sem("bv_ready")
        parts_ready, brow_in = sem("parts_ready"), sem("brow_in")
        consts_ready, link1, w_steps = sem("consts_ready"), sem("link1"), sem("w_steps")
        front_done, back_done = sem("front_done"), sem("back_done")
        hi_ready, lo_ready = sem("hi_ready"), sem("lo_ready")
        mix_done, h_ready, st_ready, mv_ready, cf_ready = (sem(n) for n in ("mix_done", "h_ready", "st_ready", "mv_ready", "cf_ready"))
        veps_ready, rs_ready, st_txt, mv_txt, nm_ready = (sem(n) for n in ("veps_ready", "rs_ready", "st_txt", "mv_txt", "nm_ready"))
        txt_tiles = TILES - IMG_TILES
        early = IMG_TILES - 8

        lots = []

        def coefficients(pool, lo, hi, need):
            lots.append(lo)
            n = len(lots)
            pool.wait_ge(cf_ready, need)
            mean, rs, nm = (cf_all[:, lo:hi, k:k + 1].squeeze(2) for k in (MEAN, RS, NM))
            nc.gpsimd.tensor_tensor(rs, rs, ln_eps[:, :].to_broadcast([P, hi - lo]), ALU.add)
            nc.gpsimd.tensor_scalar(nm, mean, -1.0, None, ALU.mult).then_inc(veps_ready, 1)
            pool.wait_ge(veps_ready, n)
            nc.gpsimd.tensor_tensor(rs, rs, neghalf[:, lo:hi], ALU.pow).then_inc(rs_ready, 1)
            pool.wait_ge(rs_ready, n)
            nc.gpsimd.tensor_tensor(nm, nm, rs, ALU.mult).then_inc(nm_ready, 1)
            pool.wait_ge(nm_ready, n)

        with nc.Block() as block:
            @block.sync
            def _(sp):
                sp.dma_start(ident[:, :], ident_c).then_inc(c_in, 16)
                sp.dma_start(xbuf[0][:, :], x[0:P, :]).then_inc(x_in[0], 16)
                for b in range(1, XB):
                    if b == 2:
                        sp.wait_ge(tokw_in, 16 * (XC // 2 + 1))
                    sp.dma_start(xbuf[b][:, :], x[b * P:(b + 1) * P, :]).then_inc(x_in[b], 16)
                with sp.Fori(1, IMG_TILES // XB) as g:
                    for b in range(XB):
                        sp.wait_ge(back_done, (g - 1) * XB + b + 1)
                        sp.dma_start(xbuf[b][:, :], x[bass.ds(g * (XB * P) + b * P, P), :]).then_inc(x_in[b], 16)
                sp.wait_ge(parts_ready, 3)
                for k in range(3):
                    sp.dma_start(brow[k:k + 1, :], bias_p[k][:, :]).then_inc(brow_in, 16)
                sp.wait_ge(brow_in, 16 * 3)

            @block.scalar
            def _(act):
                for c in range(XC):
                    if c % 2 == 0:
                        act.dma_start(tokw[:, c:c + 2, :], ws_rep[:, c:c + 2, :]).then_inc(tokw_in, 16)
                    if c == 0:
                        act.dma_start(tokd[:, :], w_rep).then_inc(tokw_in, 16)
                act.wait_ge(consts_ready, 1)
                nc.scalar.activation(warm[:, :], ln_eps[:, :], ACT.Copy)
                def high(i, p):
                    wait(act, mix_done, i - 1)
                    act.wait_ge(front_done, i + 1)
                    nc.scalar.activation(x_t[p][0][:, 0:4, :], bank[2 * p][:, :], ACT.Copy).then_inc(hi_ready, 1)
                    act.wait_ge(back_done, i + 1)
                    nc.scalar.activation(x_t[p][0][:, 4:8, :], bank[2 * p + 1][:, :], ACT.Copy).then_inc(hi_ready, 1)

                for b in range(2):
                    high(b, b % 2)
                for c in range(0, XC, 2):
                    act.wait_ge(tokw_f, c // 2 + 1)
                    nc.scalar.activation(tokw_h[:, c:c + 2, :], tokw[:, c:c + 2, :], ACT.Copy).then_inc(tokw_hi, 1)
                full = TILES - 1 - IMG_TILES
                act.wait_ge(txt_zero, 1)
                act.dma_start(h_all[:, IMG_TILES:TILES - 1, :],
                              txt[0:full * P, :].rearrange("(n p) f -> p n f", p=P)).then_inc(txt_in, 16)
                act.dma_start(h_all[0:TAIL, TILES - 1, :], txt[full * P:full * P + TAIL, :]).then_inc(txt_in, 16)
                for dst, src in ((bv_s[:, :], bv), (bo_s[:, :], bo.unsqueeze(0).to_broadcast([P, D])),
                                 (bq_s[:, :], bq.unsqueeze(0).to_broadcast([P, D])), (bias_f[:, :], biases), (bias_s[:, :], bscale_c), (ls[:, :], logit.unsqueeze(0).to_broadcast([P, H]))):
                    act.dma_start(dst, src).then_inc(b_in, 16)
                weights = (
                    (inw[:, :, :], in_w.rearrange("(c p) n -> p c n", p=P)),
                    (outw[:, :, :], out_w.rearrange("(c p) n -> p c n", p=P)),
                    (headw[:, :], head),
                    (wq_s[:, :, :], wq.rearrange("(c p) n -> p c n", p=P)),
                    (wd_s[:, :, :], wd.rearrange("(c p) n -> p c n", p=P)),
                    (wu_s[0:LAT, :], wu),
                    (wu_s[LAT:LAT + 1, :], bu.unsqueeze(0)),
                    (wo_s[:, :, :], wo.rearrange("(c p) n -> p c n", p=P)),
                    (wg_s[:, :, :], wg.rearrange("(c p) n -> p c n", p=P)),
                    (we_s[:, 0, :, :], we[:, 0:P, :].rearrange("e p f -> p e f")),
                    (we_s[:, 1, :, :], we[:, P:D, :].rearrange("e p f -> p e f")),
                    (g1_s[:, :], g1), (g2_s[:, :], g2),
                    (bd_s[:, :], bd.unsqueeze(1)),
                    (am_f[:, :], amask_c), (fm_f[:, :], fmask_c),
                )

                assert len(weights) == 4 * XB
                for b in range(XB):
                    if b >= 2:
                        high(b, b % 2)
                    for dst, src in weights[4 * b:4 * b + 4]:
                        act.dma_start(dst, src).then_inc(w_in, 16)
                with act.Fori(1, IMG_TILES // XB) as g:
                    for b in range(XB):
                        high(g * XB + b, b % 2)

            @block.gpsimd
            def _(pool):
                nc.gpsimd.memset(h_all[96:128, TILES - 1, :], 0.0).then_inc(txt_zero, 1)
                pool.wait_ge(txt_zero, 1)
                nc.gpsimd.memset(neghalf[:, :], -0.5)
                nc.gpsimd.memset(onehalf[:, :], 1.5)
                nc.gpsimd.memset(ln_eps[:, :], LN_EPS)
                nc.gpsimd.memset(rms_eps[:, :], RMS_EPS)
                nc.gpsimd.memset(one_s[:, :], 1.0)
                nc.gpsimd.memset(ones3[:, :], 1.0)
                nc.gpsimd.memset(plain_mv[:, :], 1.0)
                nc.gpsimd.memset(mixed_mv[:, 0:1], 1.0 / WS)
                nc.gpsimd.memset(mixed_mv[:, 1:2], 1.0 / WS ** 2)
                nc.gpsimd.memset(kpad[:, :, :, :], 0.0)
                nc.gpsimd.memset(qpad[:, :, :], 0.0)
                for p in range(3):
                    nc.gpsimd.memset(vaug[p][:, :, HD:HD + 1], 1.0)
                for p in range(2):
                    nc.gpsimd.memset(v48[p][:, :, 33:48], 0.0)
                    last = nc.gpsimd.memset(v48[p][:, :, 32:33], 1.0)
                last.then_inc(consts_ready, 1)
                pool.wait_ge(consts_ready, 1)
                nc.gpsimd.memset(lat[LAT:LAT + 1, :], 1.0).then_inc(consts_ready, 1)
                pool.wait_ge(consts_ready, 2)
                pool.wait_ge(b_in, 16 * 6)
                wide = bv_s[:, :].unsqueeze(2).to_broadcast([P, KC, P])
                nc.gpsimd.tensor_copy(bv_h[:, :, :], wide).then_inc(bv_ready, 1)
                pool.wait_ge(bv_ready, 1)
                nc.gpsimd.tensor_tensor(bv_l[:, :, :], wide, bv_h[:, :, :], ALU.subtract).then_inc(bv_ready, 1)
                pool.wait_ge(w_in, 16 * 16)
                todo = [(w, w_h, w_l, gain, scale, c)
                        for w, w_h, w_l, gain, scale in ((inw, inw_h, inw_l, one_s, WS), (outw, outw_h, outw_l, headw, WS),
                                                         (wq_s, wq_h, wq_l, g1_s, WS), (wd_s, wd_h, wd_l, g1_s, WS),
                                                         (wo_s, wo_h, wo_l, one_s, WS), (wg_s, wg_h, wg_l, g2_s, 1.0),
                                                         (we_s, we_h, we_l, g2_s, WS))
                        for c in range(KC)]
                for w, _, _, gain, scale, c in todo:
                    last = nc.gpsimd.tensor_scalar(w[:, c], w[:, c], gain[:, c:c + 1], scale, ALU.mult, ALU.mult)
                last.then_inc(w_steps, 1)
                pool.wait_ge(w_steps, 1)
                nc.gpsimd.tensor_copy(wu_h[:, :], wu_s[:, :])
                for w, w_h, _, _, _, c in todo:
                    last = nc.gpsimd.tensor_copy(w_h[:, c], w[:, c])
                last.then_inc(w_steps, 1)
                pool.wait_ge(w_steps, 2)
                nc.gpsimd.tensor_tensor(wu_l[:, :], wu_s[:, :], wu_h[:, :], ALU.subtract)
                for w, w_h, w_l, _, _, c in todo:
                    nc.gpsimd.tensor_tensor(w_l[:, c], w[:, c], w_h[:, c], ALU.subtract)
                nc.gpsimd.tensor_copy(am[:, :], am_f[:, :])
                nc.gpsimd.tensor_copy(fm[:, :], fm_f[:, :]).then_inc(consts_ready, 1)

                coefficients(pool, IMG_TILES, TILES, txt_tiles + XB)
                coefficients(pool, 0, early, txt_tiles + early)

            @block.vector
            def _(dve):
                def low(i, p):
                    for half in range(2):
                        dve.wait_ge(hi_ready, i * 2 + half + 1)
                        nc.vector.tensor_tensor(x_t[p][1][:, 4 * half:4 * half + 4, :], bank[2 * p + half][:, :],
                                                x_t[p][0][:, 4 * half:4 * half + 4, :], ALU.subtract).then_inc(lo_ready, 1)

                for b in range(2):
                    low(b, b % 2)
                dve.wait_ge(tokw_in, 16 * (XC // 2 + 1))
                for c in range(0, XC, 2):
                    nc.vector.scalar_tensor_tensor(out=tokw[:, c:c + 2, :], in0=tokw[:, c:c + 2, :], scalar=WS,
                                                   in1=tokd[:, :].unsqueeze(1).to_broadcast([P, 2, D]),
                                                   op0=ALU.mult, op1=ALU.mult).then_inc(tokw_f, 1)
                for c in range(0, XC, 2):
                    dve.wait_ge(tokw_hi, c // 2 + 1)
                    nc.vector.tensor_tensor(tokw_l[:, c:c + 2, :], tokw[:, c:c + 2, :], tokw_h[:, c:c + 2, :],
                                            ALU.subtract).then_inc(tokw_ready, 1)

                def stats(row, taken):
                    nc.vector.bn_stats(st[:, :], row).then_inc(taken, 1)

                def stats_kept(n, at, unscale, taken, together):
                    settle(dve, tokw_ready)
                    dve.wait_ge(taken, n)
                    nc.vector.bn_aggr(mv[:, :], st[:, :]).then_inc(together, 1)
                    dve.wait_ge(together, n)
                    nc.vector.tensor_tensor(at, mv[:, :], unscale[:, :], ALU.mult).then_inc(cf_ready, 1)

                def take(i, p):
                    dve.wait_ge(mix_done, i + 1)
                    stats(bank[4 + p][:, 0:D], st_ready)
                    nc.vector.tensor_scalar(h_all[:, bass.ds(i, 1), :].squeeze(1), bank[4 + p][:, 0:D], 1.0 / WS, None,
                                            ALU.mult).then_inc(h_ready, 1)
                    stats_kept(i + 1, cf_all[:, bass.ds(i, 1), 0:2].squeeze(1), mixed_mv, st_ready, mv_ready)

                def text(n):
                    stats(h_all[:, IMG_TILES + n, :], st_txt)
                    stats_kept(n + 1, cf_all[:, IMG_TILES + n, 0:2], plain_mv, st_txt, mv_txt)

                for b in range(XB):
                    if b >= 2:
                        low(b, b % 2)
                    if b:
                        take(b - 1, (b - 1) % 2)
                        if b == 1:
                            dve.wait_ge(txt_in, 32)
                            dve.wait_ge(consts_ready, 2)
                        for n in (range(b - 1, b) if b < XB - 1 else range(b - 1, txt_tiles)):
                            text(n)
                dve.wait_ge(b_in, 16 * 6)
                n = 0

                def linked(op):
                    nonlocal n
                    n += 1
                    op.then_inc(link1, 1)
                    dve.wait_ge(link1, n)

                linked(nc.vector.tensor_tensor(bias_l[0][:, :], bias_f[:, :], bias_s[:, :], ALU.mult))
                for k in range(3):
                    nc.vector.tensor_copy(bias_p[k][:, :], bias_l[k][:, :]).then_inc(parts_ready, 1)
                    dve.wait_ge(parts_ready, k + 1)
                    if k < 2:
                        linked(nc.vector.tensor_tensor(bias_l[k + 1][:, :], bias_l[k][:, :], bias_p[k][:, :], ALU.subtract))
                nc.vector.tensor_scalar(ls[:, :], ls[:, :], 4.605170185988091, None, ALU.min).then_inc(ls_min, 1)
                with dve.Fori(1, IMG_TILES // XB) as g:
                    for b in range(XB):
                        low(g * XB + b, b % 2)
                        take(g * XB + b - 1, (b - 1) % 2)
                take(IMG_TILES - 1, (IMG_TILES - 1) % 2)

            @block.tensor
            def _(pe):
                def turn(i, p, b, full):
                    pe.wait_ge(x_in[b], full)
                    for c in range(XC):
                        half = nc.tensor.transpose(bank[2 * p + c // 4][:, (c % 4) * P:(c % 4 + 1) * P],
                                                   xbuf[b][:, c * P:(c + 1) * P], ident[:, :])
                        if c == 3:
                            half.then_inc(front_done, 1)
                    half.then_inc(back_done, 1)

                def mix(i, p):
                    pe.wait_ge(lo_ready, i * 2 + 2)
                    wait(pe, h_ready, i - 1)
                    t_h, t_l = x_t[p]
                    product(bank[4 + p][:, 0:D], lambda c: t_h[:, c, :], lambda c: t_l[:, c, :],
                            lambda c: tokw_h[:, c, :], lambda c: tokw_l[:, c, :], XC).then_inc(mix_done, 1)

                pe.wait_ge(c_in, 16)
                for b in range(XB):
                    turn(b, b % 2, b, 16)
                    if b == 1:
                        pe.wait_ge(tokw_ready, XC // 2)
                    if b:
                        mix(b - 1, (b - 1) % 2)
                with pe.Fori(1, IMG_TILES // XB) as g:
                    for b in range(XB):
                        turn(g * XB + b, b % 2, b, g * 16 + 16)
                        mix(g * XB + b - 1, (b - 1) % 2)
                mix(IMG_TILES - 1, (IMG_TILES - 1) % 2)

        phase1.close()
        xn = sb("xn", [P, D])
        xt_h, xt_l = halves("xt", [P, KC, P])
        sq = sb("sq", [P, 2 * H, HD])
        ss = sb("ss", [P, 2 * H])
        half_ss = sb("half_ss", [P, 2 * H])
        shifted = sb("shifted", [P, 2 * H])
        rn = sb("rn", [P, 2 * H])
        rt = sb("rt", [P, 2 * H])
        qkr = [sb(f"qkr{p}", [P, 2 * D]) for p in range(3)]
        qn = sb("qn", [P, H, HD])
        q_t = sb("q_t", [P, 8, 32])
        k_t = sb("k_t", [P, 8, 64])
        smax = sb("smax", [P, 16])
        sc = sb("sc", [P, 16, 32])
        pr = sb("pr", [P, 16, 32])
        pr_t = [sb(f"pr_t{p}", [P, 16, 32]) for p in range(3)]
        rsum = sb("rsum", [P, H])
        on = sb("on", [P, H, HD])
        on_h, on_l = halves("on_t", [P, KC, P])
        mv3 = sb("mv3", [P, 2])
        cf = sb("cf", [P, 4])
        vtmp = sb("vtmp", [P, 1])
        ms = sb("ms", [P, 1])
        mse = sb("mse", [P, 1])
        ms2 = sb("ms2", [P, 1])
        x1 = sb("x1", [P, D])
        x1b = sb("x1b", [P, D])
        hn = sb("hn", [P, D])
        hn_h, hn_l = halves("hn_t", [P, KC, P])
        fq_t = sb("fq_t", [P, 32, H])
        kv_t = sb("kv_t", [P, H, 32])
        of = sb("of", [P, H, 32])
        x2 = sb("x2", [P, D])
        hx2 = [sb(f"hx2_{p}", [P, D]) for p in range(2)]
        junk = sb("junk", [P, D])
        ss2 = sb("ss2", [P, 1])
        t2 = sb("t2", [P, 1])
        r2 = sb("r2", [P, 1])
        h2 = sb("h2", [P, D])
        h2_t = [halves(f"h2_t{p}", [P, KC, P]) for p in range(2)]
        gmax = sb("gmax", [P, 1])
        gexp = sb("gexp", [P, E])
        gsum = sb("gsum", [P, 1])
        grec = sb("grec", [P, 1])
        gate = [sb(f"gate{p}", [P, E]) for p in range(2)]
        acc = sb("acc", [P, D])
        res = sb("res", [P, D])

        names = ("ls_ready", "a_xn", "a_xnps", "a_xth", "a_xtl", "a_qkm", "a_vm", "a_sq", "a_qkr", "a_v", "a_ss", "a_half",
                 "a_shift", "a_guess", "a_lsq", "a_qk", "a_qkt", "a_s", "a_max", "a_sub", "a_exp", "a_prt", "a_av", "a_rsum",
                 "a_on", "a_onps", "a_onh", "a_onl", "a_out", "a_h", "a_st", "a_mv", "a_keep", "p_newton", "p_rn", "p_kpad", "p_bias",
                 "bvec_ps", "bvec_ready")
        (ls_ready, a_xn, a_xnps, a_xth, a_xtl, a_qkm, a_vm, a_sq, a_qkr, a_v, a_ss, a_half,
         a_shift, a_guess, a_lsq, a_qk, a_qkt, a_s, a_max, a_sub, a_exp, a_prt, a_av, a_rsum,
         a_on, a_onps, a_onh, a_onl, a_out, a_h, a_st, a_mv, a_keep, p_newton, p_rn, p_kpad, p_bias,
         bvec_ps, bvec_ready) = map(sem, names)
        b_xt, b_qk, b_v, b_s, b_o, b_ot, b_out = bank[0:7]

        p_mv, p_var, p_rs, p_ms, p_mse, p_rms, p_rr, p_all = (
            sem(n) for n in ("p_mv", "p_var", "p_rs", "p_ms", "p_mse", "p_rms", "p_rr", "p_all"))

        def ffn_coefficients(pool, j):
            at = bass.ds(j, 1)
            nc.gpsimd.tensor_copy(mv3[:, :], cf_all[:, at, 0:2].squeeze(1)).then_inc(p_mv, 1)
            pool.wait_ge(p_mv, j + 1)
            nc.gpsimd.tensor_tensor(vtmp[:, :], mv3[:, 1:2], ln_eps[:, :], ALU.add).then_inc(p_var, 1)
            wait(pool, p_all, j)
            pool.wait_ge(p_var, j + 1)
            nc.gpsimd.tensor_tensor(cf[:, RS:RS + 1], vtmp[:, :], neghalf[:, 0:1], ALU.pow).then_inc(p_rs, 1)
            settle(pool, consts_ready)
            pool.wait_ge(p_rs, j + 1)
            nc.gpsimd.tensor_scalar(ms[:, :], mv3[:, 1:2], cf[:, RS:RS + 1], cf[:, RS:RS + 1], ALU.mult, ALU.mult)
            nc.gpsimd.tensor_copy(cf[:, MEAN:MEAN + 1], mv3[:, 0:1])
            nc.gpsimd.tensor_scalar(cf[:, NM:NM + 1], mv3[:, 0:1], cf[:, RS:RS + 1], -1.0, ALU.mult,
                                    ALU.mult).then_inc(p_ms, 1)
            pool.wait_ge(p_ms, j + 1)
            nc.gpsimd.tensor_tensor(mse[:, :], ms[:, :], rms_eps[:, :], ALU.add).then_inc(p_mse, 1)
            pool.wait_ge(p_mse, j + 1)
            nc.gpsimd.tensor_tensor(ms2[:, :], mse[:, :], neghalf[:, 0:1], ALU.pow).then_inc(p_rms, 1)
            pool.wait_ge(p_rms, j + 1)
            nc.gpsimd.tensor_tensor(cf[:, RR:RR + 1], ms2[:, :], cf[:, RS:RS + 1], ALU.mult).then_inc(p_rr, 1)
            settle(pool, consts_ready)
            pool.wait_ge(p_rr, j + 1)
            nc.gpsimd.tensor_copy(cf_all[:, at, :], cf[:, :].unsqueeze(1)).then_inc(p_all, 1)

        names = ("f_hn", "f_hnps", "f_hth", "f_htl", "f_q", "f_down", "f_lat", "f_lath", "f_latl", "f_qraw", "f_qpad", "f_kv", "f_kvt", "f_qt",
                 "f_s", "f_max", "f_sub", "f_exp", "f_prt", "f_av", "f_of", "f_rsum", "f_on", "f_onps", "f_onh", "f_onl",
                 "f_wo", "f_x2", "f_ss2", "f_h2", "f_h2ps", "f_h2h", "f_h2l", "f_gate", "f_gmax", "f_gexp", "f_grec",
                 "f_gmul", "f_we", "f_comb", "f_acc", "f_x1", "p_x1", "p_hx2", "p_t2", "p_r2", "out_done")
        (f_hn, f_hnps, f_hth, f_htl, f_q, f_down, f_lat, f_lath, f_latl, f_qraw, f_qpad, f_kv, f_kvt, f_qt,
         f_s, f_max, f_sub, f_exp, f_prt, f_av, f_of, f_rsum, f_on, f_onps, f_onh, f_onl,
         f_wo, f_x2, f_ss2, f_h2, f_h2ps, f_h2h, f_h2l, f_gate, f_gmax, f_gexp, f_grec,
         f_gmul, f_we, f_comb, f_acc, f_x1, p_x1, p_hx2, p_t2, p_r2, out_done) = map(sem, names)
        b_turn, b_q, b_kv, b_we, b_s3, b_o3, b_hn = bank[0], bank[1], bank[2], bank[3:5], bank[5], bank[6], bank[7]
        b_down, b_gate, b_wo = b_turn[0:LAT, D:D + P], b_q[:, D:D + E], b_hn[:, 0:D]
        EP = 2
        STEPS = E // EP

        def ffn_pe(pe):
            def experts(i, p, s):
                if real(i, -2):
                    wait(pe, f_comb, (i - 2) * STEPS + s - 1)
                    rows_times(b_we[s % 2][:, :], *h2_t[p], lambda c: we_h[:, c, s * EP:(s + 1) * EP, :],
                               lambda c: we_l[:, c, s * EP:(s + 1) * EP, :]).then_inc(f_we, 1)

            def scores(pairs):
                for pair in pairs:
                    for j in range(4):
                        q = slice(32 * j, 32 * j + 32)
                        last = nc.tensor.matmul(b_s3[q, pair * 32:pair * 32 + 32],
                                                fq_t[q, 2 * pair:2 * pair + 2, :].rearrange("r t h -> r (t h)"),
                                                kv_t[q, :, 2 * pair:2 * pair + 2],
                                                start=False, stop=True, skip_group_check=True)
                return last

            def sums(pairs, p):
                for pair in pairs:
                    for j in range(4):
                        q = slice(32 * j, 32 * j + 32)
                        last = nc.tensor.matmul(b_o3[q, pair * 32:pair * 32 + 32], v48[p][q, pair, 16:48],
                                                pr_t[0][q, pair, :], start=True, stop=True)
                return last

            def body(i, p):
                if real(i, 0):
                    pe.wait_ge(f_qt, i + 1)
                    nc.tensor.matmul(b_s3[:, :], fm[:, 0:P], fm[:, P:], start=True, stop=True,
                                     skip_group_check=True)
                    scores(range(0, 8))
                if real(i, -1):
                    pe.wait_ge(f_on, i)
                    wait(pe, f_h2l, i - 1)
                    if real(i, 0):
                        pe.wait_ge(f_lat, i + 1)
                    for c in range(KC):
                        last = nc.tensor.transpose(b_turn[:, c * P:(c + 1) * P],
                                                   on[:, :, :].rearrange("p h d -> p (h d)")[:, c * P:(c + 1) * P],
                                                   ident[:, :])
                    last.then_inc(f_onps, 1)
                if real(i, 1):
                    pe.wait_ge(f_htl, i + 2)
                    wait(pe, f_gexp, i - 1)
                    rows_times(b_q[:, 0:D], hn_h, hn_l, lambda c: wq_h[:, c, :],
                               lambda c: wq_l[:, c, :]).then_inc(f_q, 1)
                if real(i, 0):
                    scores(range(8, 16)).then_inc(f_s, 1)
                experts(i, p, 0)
                if real(i, 1):
                    wait(pe, f_onl, i)
                    product(b_down, lambda c: wd_h[:, c, :], lambda c: wd_l[:, c, :], lambda c: hn_h[:, c, :],
                            lambda c: hn_l[:, c, :], KC).then_inc(f_down, 1)
                experts(i, p, 1)
                if real(i, -1):
                    pe.wait_ge(f_onl, i)
                    rows_times(b_wo, on_h, on_l, lambda c: wo_h[:, c, :], lambda c: wo_l[:, c, :]).then_inc(f_wo, 1)
                if real(i, 1):
                    pe.wait_ge(f_latl, i + 2)
                    wait(pe, f_kvt, i + 1)
                    nc.tensor.matmul(b_kv[:, :], lat_h[:, :], wu_h[:, :], start=True, stop=False)
                    nc.tensor.matmul(b_kv[:, :], lat_h[:, :], wu_l[:, :], start=False, stop=False)
                    nc.tensor.matmul(b_kv[:, :], lat_l[:, :], wu_h[:, :], start=False, stop=True).then_inc(f_kv, 1)
                if real(i, 0):
                    settle(pe, c_in)
                    pe.wait_ge(f_prt, i + 1)
                    wait(pe, f_of, i)
                    sums(range(0, 8), p)
                experts(i, p, 2)
                if real(i, 0):
                    sums(range(8, 16), p).then_inc(f_av, 1)
                if real(i, -1):
                    pe.wait_ge(f_h2, i)
                    for c in range(KC):
                        last = nc.tensor.transpose(b_turn[:, c * P:(c + 1) * P], h2[:, c * P:(c + 1) * P], ident[:, :])
                    last.then_inc(f_h2ps, 1)
                if real(i, 2):
                    pe.wait_ge(f_hn, i + 3)
                    wait(pe, f_x2, i)
                    for c in range(KC):
                        last = nc.tensor.transpose(b_hn[:, c * P:(c + 1) * P], hn[:, c * P:(c + 1) * P], ident[:, :])
                    last.then_inc(f_hnps, 1)
                experts(i, p, 3)
                if real(i, -1):
                    pe.wait_ge(f_h2l, i)
                    if real(i, 1):
                        pe.wait_ge(f_qraw, i + 2)
                    rows_times(b_gate, *h2_t[1 - p], lambda c: wg_h[:, c, :], lambda c: wg_l[:, c, :],
                               slice(6 * D, 6 * D + E)).then_inc(f_gate, 1)

            return body

        def ffn_act(act):
            def body(i, p):
                if real(i, -1):
                    act.wait_ge(f_onps, i)
                    wait(act, f_wo, i - 1)
                    nc.scalar.activation(on_h[:, :, :], b_turn[:, 0:D], ACT.Copy).then_inc(f_onh, 1)
                if real(i, 1):
                    act.wait_ge(f_q, i + 2)
                    wait(act, f_qpad, i + 1)
                    nc.scalar.activation(qraw[:, :], b_q[:, 0:D], ACT.Copy, scale=1.0 / WS).then_inc(f_qraw, 1)
                if real(i, 0):
                    act.wait_ge(f_sub, i + 1)
                    wait(act, f_prt, i)
                    nc.scalar.activation(pr[:, :, :], sc[:, :, :], ACT.Exp, scale=HD ** -0.5).then_inc(f_exp, 1)
                if real(i, 1):
                    act.wait_ge(f_down, i + 2)
                    wait(act, f_latl, i + 1)
                    nc.scalar.activation(lat[0:LAT, :], b_down, ACT.Identity, bias=bd_s[:, :],
                                         scale=1.0 / WS).then_inc(f_lat, 1)
                    act.wait_ge(f_lat, i + 2)
                    wait(act, f_kv, i + 1)
                    nc.scalar.activation(lat_h[:, :], lat[:, :], ACT.Copy).then_inc(f_lath, 1)
                if real(i, -1):
                    act.wait_ge(f_x2, i)
                    wait(act, p_t2, i - 1)
                    nc.scalar.activation(junk[:, :], x2[:, :], ACT.Square, scale=D ** -0.5,
                                         accum_out=ss2[:, :]).then_inc(f_ss2, 1)
                if real(i, 0):
                    settle(act, ls_ready)
                    wait(act, p_x1, i)
                    act.wait_ge(p_all, i + 1)
                    at = bass.ds(i, 1)
                    nc.scalar.activation(x1[:, :], h_all[:, at, :].squeeze(1), ACT.Identity,
                                         bias=cf_all[:, at, NM:NM + 1].squeeze(1),
                                         scale=cf_all[:, at, RS:RS + 1].squeeze(1)).then_inc(f_x1, 1)
                if real(i, -1):
                    act.wait_ge(f_h2ps, i)
                    wait(act, f_gate, i - 2)
                    wait(act, f_we, (i - 2) * STEPS)
                    nc.scalar.activation(h2_t[1 - p][0][:, :, :], b_turn[:, 0:D], ACT.Copy).then_inc(f_h2h, 1)
                if real(i, 2):
                    act.wait_ge(f_hnps, i + 3)
                    wait(act, f_down, i + 2)
                    nc.scalar.activation(hn_h[:, :, :], b_hn[:, 0:D], ACT.Copy).then_inc(f_hth, 1)
                if real(i, -1):
                    act.wait_ge(f_gmax, i)
                    wait(act, f_gmul, i - 1)
                    nc.scalar.activation(gexp[:, :], b_gate, ACT.Exp, bias=gmax[:, :],
                                         accum_out=gsum[:, :]).then_inc(f_gexp, 1)

            return body

        def ffn_dve(dve):
            def combine(i, p, s):
                if not real(i, -2):
                    return
                dve.wait_ge(f_we, (i - 2) * STEPS + s + 1)
                if s == 0:
                    dve.wait_ge(f_gmul, i - 1)
                    dve.wait_ge(p_hx2, i - 1)
                else:
                    dve.wait_ge(f_comb, (i - 2) * STEPS + s)
                for k in range(EP):
                    e = s * EP + k
                    if k:
                        dve.wait_ge(f_acc, (i - 2) * STEPS + s + 1)
                    if e == E - 1:
                        wait(dve, out_done, (i - 2) * 16)
                    op = nc.vector.scalar_tensor_tensor(
                        out=(res if e == E - 1 else acc)[:, :], in0=b_we[s % 2][:, k * D:(k + 1) * D],
                        scalar=gate[p][:, e:e + 1], in1=(acc if e else hx2[p])[:, :], op0=ALU.mult, op1=ALU.add)
                    op.then_inc(f_comb if k else f_acc, 1)

            def body(i, p):
                if real(i, -1):
                    dve.wait_ge(f_onh, i)
                    nc.vector.tensor_tensor(on_l[:, :, :], b_turn[:, 0:D], on_h[:, :, :], ALU.subtract).then_inc(f_onl, 1)
                if real(i, 0):
                    dve.wait_ge(f_s, i + 1)
                    s3 = b_s3[:, :].rearrange("p (h m) -> p h m", m=32)
                    nc.vector.tensor_reduce(smax[:, :], s3, AX.X, ALU.max).then_inc(f_max, 1)
                    dve.wait_ge(f_max, i + 1)
                    wait(dve, f_exp, i)
                    nc.vector.tensor_tensor(sc[:, :, :], s3, smax[:, :].unsqueeze(2).to_broadcast([P, 16, 32]),
                                            ALU.subtract).then_inc(f_sub, 1)
                combine(i, p, 0)
                if real(i, 1):
                    dve.wait_ge(f_lath, i + 2)
                    wait(dve, f_kv, i + 1)
                    nc.vector.tensor_tensor(lat_l[:, :], lat[:, :], lat_h[:, :], ALU.subtract).then_inc(f_latl, 1)
                if real(i, 0):
                    dve.wait_ge(f_exp, i + 1)
                    wait(dve, f_av, i)
                    nc.vector.transpose(pr_t[0][:, :, :], pr[:, :, :]).then_inc(f_prt, 1)
                combine(i, p, 1)
                if real(i, -1):
                    dve.wait_ge(f_wo, i)
                    dve.wait_ge(p_x1, i)
                    wait(dve, p_hx2, i - 1)
                    wait(dve, f_ss2, i - 1)
                    nc.vector.scalar_tensor_tensor(out=x2[:, :], in0=b_wo, scalar=1.0 / WS, in1=x1b[:, :],
                                                   op0=ALU.mult, op1=ALU.add).then_inc(f_x2, 1)
                if real(i, 1):
                    dve.wait_ge(f_qpad, i + 2)
                    nc.vector.transpose(fq_t[:, :, :].rearrange("r t h -> r h t"), qpad[:, :, :])
                    dve.wait_ge(f_kv, i + 2)
                    nc.vector.transpose(kv_t[:, :, :], b_kv[:, :]).then_inc(f_kvt, 1)
                    dve.wait_ge(f_kvt, i + 2)
                if real(i, 1):
                    nc.vector.transpose(v48[1 - p][:, :, 0:32],
                                        kv_t[:, :, :].rearrange("r g (p t) -> r p g t", t=2)).then_inc(f_qt, 1)
                if real(i, -1):
                    dve.wait_ge(p_r2, i)
                    wait(dve, f_h2ps, i - 1)
                    nc.vector.tensor_scalar(h2[:, :], x2[:, :], r2[:, :], None, ALU.mult).then_inc(f_h2, 1)
                combine(i, p, 2)
                if real(i, 0):
                    dve.wait_ge(f_av, i + 1)
                    nc.vector.transpose(of[:, :, :], b_o3[:, :].rearrange("r (t h) -> r h t", h=H)).then_inc(f_of, 1)
                    dve.wait_ge(f_of, i + 1)
                    nc.vector.reciprocal(rsum[:, :], of[:, :, HD:HD + 1]).then_inc(f_rsum, 1)
                if real(i, -1):
                    dve.wait_ge(f_h2h, i)
                    nc.vector.tensor_tensor(h2_t[1 - p][1][:, :, :], b_turn[:, 0:D], h2_t[1 - p][0][:, :, :],
                                            ALU.subtract).then_inc(f_h2l, 1)
                if real(i, 0):
                    dve.wait_ge(f_rsum, i + 1)
                    wait(dve, f_onps, i)
                    nc.vector.tensor_tensor(on[:, :, :], of[:, :, 0:HD], rsum[:, :].unsqueeze(2).to_broadcast([P, H, HD]),
                                            ALU.mult).then_inc(f_on, 1)
                if real(i, 2):
                    dve.wait_ge(f_hth, i + 3)
                    nc.vector.tensor_tensor(hn_l[:, :, :], b_hn[:, 0:D], hn_h[:, :, :], ALU.subtract).then_inc(f_htl, 1)
                if real(i, 3):
                    settle(dve, tokw_ready)
                    wait(dve, f_hnps, i + 3)
                    dve.wait_ge(p_all, i + 4)
                    at = bass.ds(i + 3, 1)
                    nc.vector.tensor_scalar(hn[:, :], h_all[:, at, :].squeeze(1), cf_all[:, at, MEAN:MEAN + 1].squeeze(1),
                                            cf_all[:, at, RR:RR + 1].squeeze(1), ALU.subtract, ALU.mult).then_inc(f_hn, 1)
                if real(i, -1):
                    dve.wait_ge(f_gate, i)
                    nc.vector.tensor_reduce(gmax[:, :], b_gate, AX.X, ALU.max, negate=True).then_inc(f_gmax, 1)
                combine(i, p, 3)
                if real(i, -1):
                    dve.wait_ge(f_gexp, i)
                    nc.vector.reciprocal(grec[:, :], gsum[:, :]).then_inc(f_grec, 1)
                    dve.wait_ge(f_grec, i)
                    nc.vector.tensor_scalar(gate[1 - p][:, :], gexp[:, :], grec[:, :], 1.0 / WS, ALU.mult,
                                            ALU.mult).then_inc(f_gmul, 1)

            return body

        def ffn_pool(pool):
            def body(i, p):
                if real(i, 1):
                    pool.wait_ge(f_qraw, i + 2)
                    wait(pool, f_qt, i + 1)
                    nc.gpsimd.tensor_tensor(qpad[:, :, 0:HD], qraw[:, :].rearrange("p (h d) -> p h d", d=HD),
                                            bq_s[:, :].rearrange("p (h d) -> p h d", d=HD), ALU.add).then_inc(f_qpad, 1)
                if real(i, AHEAD) and real(i, 0):
                    ffn_coefficients(pool, i + AHEAD)
                if real(i, -1):
                    pool.wait_ge(f_ss2, i)
                    nc.gpsimd.tensor_tensor(t2[:, :], ss2[:, :], rms_eps[:, :], ALU.add).then_inc(p_t2, 1)
                    pool.wait_ge(p_t2, i)
                    wait(pool, f_h2, i - 1)
                    nc.gpsimd.tensor_tensor(r2[:, :], t2[:, :], neghalf[:, 0:1], ALU.pow).then_inc(p_r2, 1)
                    settle(pool, consts_ready)
                    wait(pool, f_acc, (i - 3) * STEPS + 1)
                    nc.gpsimd.tensor_tensor(hx2[1 - p][:, :], h_all[:, bass.ds(i - 1, 1), :].squeeze(1), x2[:, :],
                                            ALU.add).then_inc(p_hx2, 1)
                if real(i, 0):
                    pool.wait_ge(f_x1, i + 1)
                    wait(pool, f_x2, i)
                    nc.gpsimd.tensor_tensor(x1b[:, :], x1[:, :], bo_s[:, :], ALU.add).then_inc(p_x1, 1)

            return body

        with nc.Block() as block:
            @block.tensor
            def _(pe):
                def sums(i, p, half):
                    if not real(i, -1):
                        return
                    if half == 0:
                        settle(pe, c_in)
                        pe.wait_ge(a_prt, i)
                        pe.wait_ge(a_v, i)
                    for h in range(half * 8, half * 8 + 8):
                        for j in range(4):
                            q = slice(32 * j, 32 * j + 32)
                            last = nc.tensor.matmul(b_o[q, h * 17:h * 17 + 17], pr_t[(p + 2) % 3][q, h, :],
                                                    vaug[(p + 2) % 3][q, h, :], start=True, stop=True)
                    if half == 1:
                        last.then_inc(a_av, 1)

                def scores(pairs):
                    for pair in pairs:
                        for j in range(4):
                            q = slice(32 * j, 32 * j + 32)
                            last = nc.tensor.matmul(b_s[q, pair * 64:pair * 64 + 64], q_t[q, pair, :], k_t[q, pair, :],
                                                    start=False, stop=True, skip_group_check=True)
                    return last

                def body(i, p):
                    if real(i, 0):
                        pe.wait_ge(a_qkt, i + 1)
                        wait(pe, a_sub, i)
                        nc.tensor.matmul(b_s[:, :], am[:, 0:P], am[:, P:], start=True, stop=True,
                                         skip_group_check=True)
                        scores(range(0, 4))
                    if real(i, 0):
                        scores(range(4, 8)).then_inc(a_s, 1)
                    if real(i, -2):
                        pe.wait_ge(a_onl, i - 1)
                        wait(pe, a_h, i - 2)
                        if isinstance(i, int) and i == 2:
                            pe.wait_ge(bvec_ready, 1)
                        rows_times(b_out[:, 0:D], on_h, on_l, lambda c: outw_h[:, c, :], lambda c: outw_l[:, c, :]).then_inc(a_out, 1)
                    if real(i, 3):
                        pe.wait_ge(a_xn, i + 4)
                        wait(pe, a_xtl, i + 3)
                        for c in range(KC):
                            last = nc.tensor.transpose(b_xt[:, c * P:(c + 1) * P], xn[:, c * P:(c + 1) * P], ident[:, :])
                        last.then_inc(a_xnps, 1)
                    sums(i, p, 0)
                    sums(i, p, 1)
                    if real(i, 2):
                        pe.wait_ge(a_xtl, i + 3)
                        wait(pe, a_qkr, i + 2)
                        rows_times(b_qk[:, :], xt_h, xt_l, lambda c: inw_h[:, c, 0:2 * D],
                                   lambda c: inw_l[:, c, 0:2 * D], slice(0, 2 * D)).then_inc(a_qkm, 1)
                    if real(i, 2):
                        wait(pe, a_v, i + 2)
                        rows_times(b_v[:, 0:D], xt_h, xt_l, lambda c: inw_h[:, c, 2 * D:3 * D],
                                   lambda c: inw_l[:, c, 2 * D:3 * D]).then_inc(a_vm, 1)
                    if real(i, -1):
                        pe.wait_ge(a_on, i)
                        for c in range(KC):
                            last = nc.tensor.transpose(b_ot[:, c * P:(c + 1) * P],
                                                       on[:, :, :].rearrange("p h d -> p (h d)")[:, c * P:(c + 1) * P],
                                                       ident[:, :])
                        last.then_inc(a_onps, 1)

                rows_times(b_out[:, 0:D], bv_h, bv_l, lambda c: outw_h[:, c, :], lambda c: outw_l[:, c, :],
                           slice(3 * D, 4 * D)).then_inc(bvec_ps, 1)
                head = ffn_pe(pe)
                tiles_in_order(pe, body, 2, 3, 3, then=lambda i: in_tail(head, i))

            @block.scalar
            def _(act):
                nc.scalar.activation(ls[:, :], ls[:, :], ACT.Exp).then_inc(ls_ready, 1)

                def body(i, p):
                    if real(i, 3):
                        settle(act, tokw_ready)
                        wait(act, a_xnps, i + 3)
                        at = bass.ds(i + 3, 1)
                        nc.scalar.activation(xn[:, :], h_all[:, at, :].squeeze(1), ACT.Identity,
                                             bias=cf_all[:, at, NM:NM + 1].squeeze(1),
                                             scale=cf_all[:, at, RS:RS + 1].squeeze(1)).then_inc(a_xn, 1)
                    if real(i, 0):
                        act.wait_ge(a_sub, i + 1)
                        wait(act, a_prt, i)
                        nc.scalar.activation(pr[:, :, :], sc[:, :, :], ACT.Exp).then_inc(a_exp, 1)
                    if real(i, 2):
                        act.wait_ge(a_qkm, i + 3)
                        wait(act, a_ss, i + 2)
                        nc.scalar.activation(sq[:, :, :], b_qk[:, :], ACT.Square, scale=1.0 / WS).then_inc(a_sq, 1)
                        wait(act, a_qk, i)
                        nc.scalar.activation(qkr[(p + 2) % 3][:, :], b_qk[:, :], ACT.Copy, scale=1.0 / WS).then_inc(a_qkr, 1)
                    if real(i, 3):
                        act.wait_ge(a_xnps, i + 4)
                        wait(act, a_vm, i + 3)
                        nc.scalar.activation(xt_h[:, :, :], b_xt[:, 0:D], ACT.Copy).then_inc(a_xth, 1)
                    if real(i, -1):
                        act.wait_ge(a_onps, i)
                        wait(act, a_out, i - 1)
                        nc.scalar.activation(on_h[:, :, :], b_ot[:, 0:D], ACT.Copy).then_inc(a_onh, 1)
                    if real(i, 2):
                        act.wait_ge(a_vm, i + 3)
                        wait(act, a_av, i)
                        nc.scalar.activation(vaug[(p + 2) % 3][:, :, 0:HD], b_v[:, 0:D], ACT.Copy, scale=1.0 / WS).then_inc(a_v, 1)

                head = ffn_act(act)
                tiles_in_order(act, body, 2, 3, 3, then=lambda i: in_tail(head, i))

            @block.vector
            def _(dve):
                s3 = b_s[:, :].rearrange("p (h m) -> p h m", h=H)
                o3 = b_o[:, 0:H * 17].rearrange("p (h d) -> p h d", d=17)

                dve.wait_ge(bvec_ps, 1)
                nc.vector.tensor_scalar(bvec[:, :], b_out[:, 0:D], 1.0 / WS, None, ALU.mult).then_inc(bvec_ready, 1)

                def body(i, p):
                    if real(i, 0):
                        dve.wait_ge(a_s, i + 1)
                        nc.vector.tensor_reduce(smax[:, :], s3, AX.X, ALU.max).then_inc(a_max, 1)
                    if real(i, -2):
                        settle(dve, tokw_ready)
                        dve.wait_ge(a_out, i - 1)
                        dve.wait_ge(p_bias, i - 1)
                        hi = h_all[:, bass.ds(i - 2, 1), :].squeeze(1)
                        nc.vector.scalar_tensor_tensor(out=hi, in0=b_out[:, 0:D], scalar=1.0 / WS, in1=hi,
                                                       op0=ALU.mult, op1=ALU.add).then_inc(a_h, 1)
                    if real(i, 0):
                        dve.wait_ge(a_max, i + 1)
                        wait(dve, a_exp, i)
                        nc.vector.tensor_tensor(sc[:, :, :], s3, smax[:, :].unsqueeze(2).to_broadcast([P, H, 32]),
                                                ALU.subtract).then_inc(a_sub, 1)
                    if real(i, -2):
                        settle(dve, tokw_ready)
                        dve.wait_ge(a_h, i - 1)
                        nc.vector.bn_stats(st[:, :], hi).then_inc(a_st, 1)
                        settle(dve, tokw_ready)
                        dve.wait_ge(a_st, i - 1)
                        nc.vector.bn_aggr(mv[:, :], st[:, :]).then_inc(a_mv, 1)
                    if real(i, 0):
                        dve.wait_ge(a_exp, i + 1)
                        nc.vector.transpose(pr_t[p][:, :, :], pr[:, :, :]).then_inc(a_prt, 1)
                    if real(i, -2):
                        settle(dve, tokw_ready)
                        dve.wait_ge(a_mv, i - 1)
                        nc.vector.tensor_copy(cf_all[:, bass.ds(i - 2, 1), 0:2].squeeze(1), mv[:, :]).then_inc(a_keep, 1)
                    if real(i, 1):
                        dve.wait_ge(p_rn, i + 2)
                        if isinstance(i, int) and i == -1:
                            dve.wait_ge(ls_ready, 1)
                        nc.vector.tensor_tensor(rn[:, 0:H], rn[:, 0:H], ls[:, :], ALU.mult).then_inc(a_lsq, 1)
                    if real(i, -1):
                        dve.wait_ge(a_av, i)
                        nc.vector.reciprocal(rsum[:, :], o3[:, :, HD:HD + 1]).then_inc(a_rsum, 1)
                    if real(i, 1):
                        dve.wait_ge(a_qkr, i + 2)
                        dve.wait_ge(a_lsq, i + 2)
                        nc.vector.tensor_tensor(qn[:, :, :], qkr[(p + 1) % 3][:, 0:D].rearrange("p (h d) -> p h d", d=HD),
                                                rn[:, 0:H].unsqueeze(2).to_broadcast([P, H, HD]),
                                                ALU.mult).then_inc(a_qk, 1)
                    if real(i, -1):
                        dve.wait_ge(a_rsum, i)
                        wait(dve, a_onps, i - 1)
                        nc.vector.tensor_tensor(on[:, :, :], o3[:, :, 0:HD], rsum[:, :].unsqueeze(2).to_broadcast([P, H, HD]),
                                                ALU.mult).then_inc(a_on, 1)
                    if real(i, 1):
                        dve.wait_ge(a_qk, i + 2)
                        nc.vector.transpose(q_t[:, :, :], qn[:, :, :])
                        dve.wait_ge(p_kpad, i + 2)
                        nc.vector.transpose(k_t[:, :, :], kpad[:, :, :, :]).then_inc(a_qkt, 1)
                    if real(i, 2):
                        dve.wait_ge(a_sq, i + 3)
                        nc.vector.tensor_reduce(ss[:, :], sq[:, :, :], AX.X, ALU.add).then_inc(a_ss, 1)
                        dve.wait_ge(a_ss, i + 3)
                        nc.vector.tensor_scalar(half_ss[:, :], ss[:, :], 1e-24, 0.5, ALU.max, ALU.mult).then_inc(a_half, 1)
                        dve.wait_ge(a_half, i + 3)
                        nc.vector.tensor_scalar(shifted[:, :].bitcast(U32), half_ss[:, :].bitcast(U32), 1, None,
                                                ALU.logical_shift_right).then_inc(a_shift, 1)
                        dve.wait_ge(a_shift, i + 3)
                        nc.vector.tensor_scalar(rn[:, :].bitcast(I32), shifted[:, :].bitcast(I32), -1.0,
                                                float(RSQRT_MAGIC - (1 << 22)), ALU.mult, ALU.add).then_inc(a_guess, 1)
                    if real(i, -1):
                        dve.wait_ge(a_onh, i)
                        wait(dve, a_out, i - 1)
                        nc.vector.tensor_tensor(on_l[:, :, :], b_ot[:, 0:D], on_h[:, :, :], ALU.subtract).then_inc(a_onl, 1)
                    if real(i, 3):
                        dve.wait_ge(a_xth, i + 4)
                        nc.vector.tensor_tensor(xt_l[:, :, :], b_xt[:, 0:D], xt_h[:, :, :], ALU.subtract).then_inc(a_xtl, 1)

                head = ffn_dve(dve)
                tiles_in_order(dve, body, 2, 3, 3, then=lambda i: in_tail(head, i))

            @block.gpsimd
            def _(pool):
                coefficients(pool, early, IMG_TILES, TILES)

                def body(i, p):
                    if real(i, 2):
                        n = 11 * (i + 2)
                        for k in range(3):
                            for m, (o, a, b, op) in enumerate(((rt, rn, rn, ALU.mult), (rt, rt, half_ss, ALU.mult),
                                                               (rt, onehalf, rt, ALU.subtract), (rn, rn, rt, ALU.mult))):
                                if k == 0 and m == 0:
                                    pool.wait_ge(a_guess, i + 3)
                                else:
                                    pool.wait_ge(p_newton, n + 4 * k + m)
                                step = nc.gpsimd.tensor_tensor(o[:, :], a[:, :], b[:, :], op)
                                step.then_inc(p_newton if (k, m) != (2, 3) else p_rn, 1)
                        raw = qkr[(p + 2) % 3]
                        settle(pool, consts_ready)
                        pool.wait_ge(a_qkr, i + 3)
                        pool.wait_ge(p_rn, i + 3)
                        wait(pool, a_qkt, i + 2)
                        nc.gpsimd.tensor_tensor(kpad[:, :, 0:4:3, :], raw[:, D:2 * D].rearrange("p (a s d) -> p a s d", s=2, d=HD),
                                                rn[:, H:].rearrange("p (a s) -> p a s", s=2).unsqueeze(3).to_broadcast([P, 8, 2, HD]),
                                                ALU.mult).then_inc(p_kpad, 1)
                    if real(i, 1):
                        if isinstance(i, int) and i == -1:
                            pool.wait_ge(bvec_ready, 1)
                        settle(pool, consts_ready)
                        pool.wait_ge(a_xn, i + 2)
                        hi = h_all[:, bass.ds(i + 1, 1), :].squeeze(1)
                        nc.gpsimd.tensor_tensor(hi, hi, bvec[:, :], ALU.add).then_inc(p_bias, 1)

                head = ffn_pool(pool)

                def then(i):
                    k = i + 1 - HEAD[0]
                    for j in range(2 * k, 2 * k + 2):
                        if 0 <= j < AHEAD:
                            pool.wait_ge(a_keep, j + 1)
                            ffn_coefficients(pool, j)
                    in_tail(head, i)

                tiles_in_order(pool, body, 2, 3, 3, then=then)

        with nc.Block() as block:
            @block.tensor
            def _(pe):
                tiles_in_order(pe, ffn_pe(pe), 2, 3, start=0)

            @block.scalar
            def _(act):
                tiles_in_order(act, ffn_act(act), 2, 3, start=0)

            @block.vector
            def _(dve):
                tiles_in_order(dve, ffn_dve(dve), 2, 3, start=0)

            @block.gpsimd
            def _(pool):
                tiles_in_order(pool, ffn_pool(pool), 2, 3, last_ahead=AHEAD, start=0)

            @block.sync
            def _(sp):
                with sp.Fori(0, TILES - 1) as i:
                    sp.wait_ge(f_comb, (i + 1) * STEPS)
                    sp.dma_start(out[bass.ds(i * P, P), :], res[:, :]).then_inc(out_done, 16)
                sp.wait_ge(f_comb, TILES * STEPS)
                sp.dma_start(out[(TILES - 1) * P:TOKENS, :], res[0:TAIL, :]).then_inc(out_done, 16)
                sp.wait_ge(out_done, TILES * 16)


def kernel(**inputs):
    import numpy as np
    import concourse.bacc as bacc
    from concourse.bass_utils import run_bass_kernel_spmd

    a = {n: np.asarray(v) for n, v in inputs.items()}

    def rows(t):
        return np.ascontiguousarray(np.swapaxes(t, 0, 1)).reshape(t.shape[0] * t.shape[1], -1)

    def columns(v):
        return v.reshape(KC, P).T

    p, c = np.arange(P), np.arange(512)

    def mask(group, of_row, of_column):
        k = np.arange(group)[:, None]
        return np.concatenate([(of_row(p) == k), (of_column(c) != k) * -BIG], axis=1).astype(np.float32)

    arrays = {
        "x": rows(a["x"].reshape(B, N_IMG, FX)), "txt": rows(a["txt"]),
        "ws_rep": np.repeat(a["L0_tok_weighted_sum"].T, 4, axis=0).reshape(XC, P, D).transpose(1, 0, 2),
        "w_rep": np.tile(a["L0_tok_weight"].T, (P // 4, 1)),
        "in_w": a["L0_attn_in_proj_weight"].T, 
        "logit": a["L0_attn_logit_scale"].reshape(H),
        "head": columns(np.repeat(a["L0_attn_head_scale"].reshape(H), HD)),
        "out_w": a["L0_attn_out_w"].T,
        "g1": columns(a["L0_ffn_gamma1"]), "wq": a["L0_ffn_Wq"],
        "wd": a["L0_ffn_Wdown"], "bd": a["L0_ffn_bdown"], "wu": a["L0_ffn_Wup"], "bu": a["L0_ffn_bup"],
        "wo": a["L0_ffn_Wo"], "g2": columns(a["L0_ffn_gamma2"]),
        "wg": a["L0_ffn_Wg"], "we": a["L0_ffn_We"],
        "ident_c": np.eye(P, dtype=np.float32),
        "amask_c": mask(4, lambda n: n % 32 // B, lambda n: n % 32 // B), "fmask_c": mask(2, lambda n: n % 32 // 16, lambda n: n % 2),
        "bv": columns(a["L0_attn_in_proj_bias"][2 * D:]), "bo": a["L0_ffn_bo"], "bq": a["L0_ffn_bq"],
        "biases": np.concatenate([a["L0_attn_in_proj_bias"], a["L0_attn_out_b"], a["L0_ffn_bq"], a["L0_ffn_bo"], a["L0_ffn_bg"],
                                  np.zeros(P * BC - NBIAS, np.float32)]).reshape(P, BC),
        "bscale_c": np.where(np.arange(P * BC) < NBIAS - E, WS, 1).astype(np.float32).reshape(P, BC),
    }
    nc = bacc.Bacc("TRN2", target_bir_lowering=False, num_devices=1)
    put, args = {}, {}
    for name, v in arrays.items():
        put[f"in_{name}"] = np.ascontiguousarray(v)
        args[name] = nc.dram_tensor(f"in_{name}", v.shape, mybir.dt.from_np(v.dtype), kind="ExternalInput").ap()
    out = nc.dram_tensor("out", (TOKENS, D), F32, kind="ExternalOutput").ap()
    build(nc, out=out, **args)
    r = run_bass_kernel_spmd(nc, [put], core_ids=[0])
    got = r.results[0]["out"].reshape(N_IMG + N_TXT, B, D)
    return np.ascontiguousarray(np.swapaxes(got, 0, 1))
```
